# Optimizing a Trainium2 kernel written in Bass

```python
import numpy as np
import jax
import jax.numpy as jnp

def _softmax(x, axis=-1):
    return jax.nn.softmax(x, axis=axis)

def _gelu(x):
    return jax.nn.gelu(x, approximate=True)

def _silu(x):
    return jax.nn.silu(x)

def _sigmoid(x):
    return jax.nn.sigmoid(x)

def _layernorm(x, axis=-1, eps=1e-05):
    m = jnp.mean(x, axis=axis, keepdims=True)
    v = jnp.var(x, axis=axis, keepdims=True)
    return (x - m) / jnp.sqrt(v + eps)

def _scatter_add(tgt, idx, src, axis=0):
    return tgt.at[idx].add(src)

def _segment_sum(src, seg, n):
    return jax.ops.segment_sum(src, seg, n)
kernel_name = 'mk_flamingo_gated_d1_seqx_r4_3d3011'

def setup_inputs(seed: int=0):
    np.random.seed(seed)
    _w = jnp.asarray

    def _rec_inputs():
        import jax
        import jax.numpy as jnp
        _rk = jax.random.key(seed)
        x = 4.136e-05 + 0.9999 * jax.random.normal(jax.random.fold_in(_rk, 1), (4, 512, 512), jnp.float32)
        _lenS = 512 - jax.random.randint(jax.random.fold_in(_rk, 7), (4,), 0, max(1, 512 // 4) + 1, jnp.int32)
        _lenS2 = 512 - jax.random.randint(jax.random.fold_in(_rk, 8), (4,), 0, max(1, 512 // 4) + 1, jnp.int32)
        _ctx_1024P = jax.random.normal(jax.random.fold_in(_rk, 11), (4, 16, 256), jnp.float32)
        _ctx_1024c = jax.random.dirichlet(jax.random.fold_in(_rk, 511), 0.3 * jnp.ones((16,), jnp.float32), (4, 512))
        _ctx_1024t = jnp.einsum('bsk,bkd->bsd', _ctx_1024c, _ctx_1024P)
        _ctx_1024t = _ctx_1024t * jax.lax.rsqrt(jnp.mean(jnp.square(_ctx_1024t)) + 1e-12) * 0.953939
        ctx_1024 = -0.000292821 + 1.00034 * (_ctx_1024t + 0.3 * jax.random.normal(jax.random.fold_in(_rk, 611), (4, 512, 256), jnp.float32))
        _g = jax.random.normal(jax.random.fold_in(_rk, 9001), (2, 1), jnp.float32)
        _g = jnp.sign(_g) * jnp.maximum(jnp.abs(_g), 1.0) + (_g == 0) * 1.0
        g_xattn = _g[0]
        g_ffn = _g[1]
        return (x, ctx_1024, g_xattn, g_ffn)
    x, ctx_1024, g_xattn, g_ffn = _rec_inputs()

    def _L0_xattn_setup():
        import jax, jax.numpy as jnp
        import numpy as np
        import math
        B, L, DM = (2, 512, 256)
        DS, DC, EXP = (16, 4, 2)
        DI = EXP * DM
        DR = math.ceil(DM / 16)
        DT_MIN, DT_MAX, DT_FLOOR = (0.001, 0.1, 0.0001)

        def _ssm_forward(hidden_states, z, in_proj_w, conv_w, conv_b, x_proj_w, dt_proj_w, dt_proj_b, A_log, D):
            b = hidden_states.shape[0]
            x = jnp.einsum('ed,bld->bel', in_proj_w, hidden_states)
            xp = jnp.pad(x, ((0, 0), (0, 0), (DC - 1, 0)))
            xc = jax.lax.conv_general_dilated(xp, conv_w[:, None, :], window_strides=(1,), padding='VALID', dimension_numbers=('NCH', 'OIH', 'NCH'), feature_group_count=DI)
            u = jax.nn.silu(xc + conv_b[None, :, None])
            x_dbl = jnp.einsum('ke,bel->bkl', x_proj_w, u)
            dt_lo = x_dbl[:, :DR]
            Bm = x_dbl[:, DR:DR + DS]
            Cm = x_dbl[:, DR + DS:]
            delta = jax.nn.softplus(jnp.einsum('er,brl->bel', dt_proj_w, dt_lo) + dt_proj_b[None, :, None])
            A = -jnp.exp(A_log)

            def step(state, xs):
                d_t, B_t, C_t, u_t = xs
                dA = jnp.exp(d_t[..., None] * A)
                state = state * dA + (d_t * u_t)[..., None] * B_t[:, None, :]
                y_t = jnp.einsum('ben,bn->be', state, C_t)
                return (state, y_t)
            xs = (jnp.moveaxis(delta, -1, 0), jnp.moveaxis(Bm, -1, 0), jnp.moveaxis(Cm, -1, 0), jnp.moveaxis(u, -1, 0))
            state0 = jnp.zeros((b, DI, DS), delta.dtype)
            _, ys = jax.lax.scan(step, state0, xs)
            y = jnp.moveaxis(ys, 0, -1)
            y = y + D[None, :, None] * u
            y = y * jax.nn.silu(z)
            return jnp.swapaxes(y, 1, 2)
        key = jax.random.key(seed)
        ks = jax.random.split(key, 8)
        hidden_states = jax.random.normal(ks[0], (B, L, DM), jnp.float32)
        z = jax.random.normal(ks[1], (B, DI, L), jnp.float32)
        in_proj_w = jax.random.normal(ks[2], (DI, DM), jnp.float32) * DM ** (-0.5)
        conv_w = jax.random.normal(ks[3], (DI, DC), jnp.float32) * DC ** (-0.5)
        conv_b = jnp.zeros((DI,), jnp.float32)
        x_proj_w = jax.random.normal(ks[4], (DR + 2 * DS, DI), jnp.float32) * DI ** (-0.5)
        dt_std = DR ** (-0.5)
        dt_proj_w = jax.random.uniform(ks[5], (DI, DR), jnp.float32, -dt_std, dt_std)
        dt = jnp.exp(jax.random.uniform(ks[6], (DI,), jnp.float32) * (math.log(DT_MAX) - math.log(DT_MIN)) + math.log(DT_MIN))
        dt = jnp.clip(dt, DT_FLOOR)
        dt_proj_b = dt + jnp.log(-jnp.expm1(-dt))
        A_log = jnp.log(jnp.broadcast_to(jnp.arange(1, DS + 1, dtype=jnp.float32), (DI, DS)))
        D = jnp.ones((DI,), jnp.float32)
        return dict(hidden_states=hidden_states, z=z, in_proj_w=in_proj_w, conv_w=conv_w, conv_b=conv_b, x_proj_w=x_proj_w, dt_proj_w=dt_proj_w, dt_proj_b=dt_proj_b, A_log=A_log, D=D)
    _L0_xattn_all = _L0_xattn_setup()
    _L0_xattn_in = {k: v for k, v in _L0_xattn_all.items() if k in ('in_proj_w', 'conv_w', 'conv_b', 'x_proj_w', 'dt_proj_w', 'dt_proj_b', 'A_log', 'D')}
    del _L0_xattn_all

    def _L0_ffn_setup():
        import jax, jax.numpy as jnp
        import numpy as np
        TOPK = 2
        key = jax.random.key(seed)
        ks = jax.random.split(key, 6)
        B, T, H, S, r, ad = (2, 1024, 512, 32, 16, 32)
        h = jax.random.normal(ks[0], (B, T, H), dtype=jnp.float32)
        Wr = jax.random.normal(ks[1], (S, H), dtype=jnp.float32) * 0.02
        U = jax.random.normal(ks[2], (S, H, r), dtype=jnp.float32) * 0.02
        V = jax.random.normal(ks[3], (S, r, H), dtype=jnp.float32) * 0.02
        attr = jax.random.normal(ks[4], (S, ad), dtype=jnp.float32) * 0.02
        Wa = jax.random.normal(ks[5], (1, ad), dtype=jnp.float32) * 0.02
        return {'h': h, 'Wr': Wr, 'U': U, 'V': V, 'attr': attr, 'Wa': Wa}
    _L0_ffn_all = _L0_ffn_setup()
    _L0_ffn_in = {k: v for k, v in _L0_ffn_all.items() if k in ('Wr', 'U', 'V', 'attr', 'Wa')}
    del _L0_ffn_all
    return {'x': x, 'ctx_1024': ctx_1024, 'g_xattn': g_xattn, 'g_ffn': g_ffn, 'L0_xattn_in_proj_w': _L0_xattn_in['in_proj_w'], 'L0_xattn_conv_w': _L0_xattn_in['conv_w'], 'L0_xattn_conv_b': _L0_xattn_in['conv_b'], 'L0_xattn_x_proj_w': _L0_xattn_in['x_proj_w'], 'L0_xattn_dt_proj_w': _L0_xattn_in['dt_proj_w'], 'L0_xattn_dt_proj_b': _L0_xattn_in['dt_proj_b'], 'L0_xattn_A_log': _L0_xattn_in['A_log'], 'L0_xattn_D': _L0_xattn_in['D'], 'L0_ffn_Wr': _L0_ffn_in['Wr'], 'L0_ffn_U': _L0_ffn_in['U'], 'L0_ffn_V': _L0_ffn_in['V'], 'L0_ffn_attr': _L0_ffn_in['attr'], 'L0_ffn_Wa': _L0_ffn_in['Wa']}

def reference(x, ctx_1024, g_xattn, g_ffn, L0_xattn_in_proj_w, L0_xattn_conv_w, L0_xattn_conv_b, L0_xattn_x_proj_w, L0_xattn_dt_proj_w, L0_xattn_dt_proj_b, L0_xattn_A_log, L0_xattn_D, L0_ffn_Wr, L0_ffn_U, L0_ffn_V, L0_ffn_attr, L0_ffn_Wa):
    import jax
    import jax.numpy as jnp

    def _L0_xattn_ref(hidden_states, z, in_proj_w, conv_w, conv_b, x_proj_w, dt_proj_w, dt_proj_b, A_log, D):
        import jax, jax.numpy as jnp
        import numpy as np
        import math
        B, L, DM = (2, 512, 256)
        DS, DC, EXP = (16, 4, 2)
        DI = EXP * DM
        DR = math.ceil(DM / 16)
        DT_MIN, DT_MAX, DT_FLOOR = (0.001, 0.1, 0.0001)

        def _ssm_forward(hidden_states, z, in_proj_w, conv_w, conv_b, x_proj_w, dt_proj_w, dt_proj_b, A_log, D):
            b = hidden_states.shape[0]
            x = jnp.einsum('ed,bld->bel', in_proj_w, hidden_states)
            xp = jnp.pad(x, ((0, 0), (0, 0), (DC - 1, 0)))
            xc = jax.lax.conv_general_dilated(xp, conv_w[:, None, :], window_strides=(1,), padding='VALID', dimension_numbers=('NCH', 'OIH', 'NCH'), feature_group_count=DI)
            u = jax.nn.silu(xc + conv_b[None, :, None])
            x_dbl = jnp.einsum('ke,bel->bkl', x_proj_w, u)
            dt_lo = x_dbl[:, :DR]
            Bm = x_dbl[:, DR:DR + DS]
            Cm = x_dbl[:, DR + DS:]
            delta = jax.nn.softplus(jnp.einsum('er,brl->bel', dt_proj_w, dt_lo) + dt_proj_b[None, :, None])
            A = -jnp.exp(A_log)

            def step(state, xs):
                d_t, B_t, C_t, u_t = xs
                dA = jnp.exp(d_t[..., None] * A)
                state = state * dA + (d_t * u_t)[..., None] * B_t[:, None, :]
                y_t = jnp.einsum('ben,bn->be', state, C_t)
                return (state, y_t)
            xs = (jnp.moveaxis(delta, -1, 0), jnp.moveaxis(Bm, -1, 0), jnp.moveaxis(Cm, -1, 0), jnp.moveaxis(u, -1, 0))
            state0 = jnp.zeros((b, DI, DS), delta.dtype)
            _, ys = jax.lax.scan(step, state0, xs)
            y = jnp.moveaxis(ys, 0, -1)
            y = y + D[None, :, None] * u
            y = y * jax.nn.silu(z)
            return jnp.swapaxes(y, 1, 2)
        return _ssm_forward(hidden_states, z, in_proj_w, conv_w, conv_b, x_proj_w, dt_proj_w, dt_proj_b, A_log, D)

    def _L0_ffn_ref(h, Wr, U, V, attr, Wa):
        import jax, jax.numpy as jnp
        import numpy as np
        TOPK = 2
        S = Wr.shape[0]
        sc = jnp.einsum('bth,sh->bts', h, Wr)
        _, idx = jax.lax.top_k(sc, TOPK)
        m = jax.nn.one_hot(idx, S, dtype=sc.dtype).sum(axis=-2)
        g = jax.nn.softmax(sc, axis=-1) * m
        g = g / (g.sum(axis=-1, keepdims=True) + 1e-08)
        hU = jnp.einsum('bth,shr->btsr', h, U)
        out = jnp.einsum('bts,btsr,srh->bth', g, hU, V)
        aw = jax.nn.sigmoid(attr @ Wa[0])
        gate = (g @ aw)[..., None]
        return out * (0.9 + 0.2 * gate)
    x = x + jnp.tanh(g_xattn[0]) * _L0_xattn_ref(ctx_1024, _layernorm(x, axis=-1), L0_xattn_in_proj_w, L0_xattn_conv_w, L0_xattn_conv_b, L0_xattn_x_proj_w, L0_xattn_dt_proj_w, L0_xattn_dt_proj_b, L0_xattn_A_log, L0_xattn_D)
    x = x + jnp.tanh(g_ffn[0]) * _L0_ffn_ref(_layernorm(x, axis=-1), L0_ffn_Wr, L0_ffn_U, L0_ffn_V, L0_ffn_attr, L0_ffn_Wa)
    return x

_drawn_inputs = setup_inputs


def setup_inputs(seed=0):
    import zlib

    import numpy as np

    out = dict(_drawn_inputs(seed))
    spreads = {'L0_xattn_conv_b': (0.0, 0.277), 'L0_xattn_D': (1.0, 0.2)}
    factors = {'L0_xattn_dt_proj_w': 6.489,
     'L0_xattn_dt_proj_b': 2.91,
     'L0_ffn_attr': 8.0,
     'L0_ffn_Wa': 8.0}
    for name, (base, spread) in spreads.items():
        noise = np.random.default_rng([zlib.crc32(name.encode()), seed]).standard_normal(out[name].shape)
        drawn = base * np.exp(spread * noise) if base else spread * noise
        out[name] = jnp.asarray(drawn.astype(out[name].dtype))
    for name, factor in factors.items():
        out[name] = (out[name] * factor).astype(out[name].dtype)
    return out
```

```python
from contextlib import ExitStack

import concourse.bass as bass
from concourse import mybir

ALU = mybir.AluOpType
ACT = mybir.ActivationFunctionType
F32 = mybir.dt.float32
I32 = mybir.dt.int32
U32 = mybir.dt.uint32

P = 128
Q = 4
EPS = 1e-5
GATE_EPS = 1e-8
START = 16


def flamingo(nc, x, ctx_t, g_xattn, g_ffn, in_w_t, conv_w, conv_b, x_w_t, dt_w_t, dt_b, a_log, d_skip,
             router_t, u_w, v_w, attr_t, attr_w, out):
    B, L, E = x.shape
    DM = ctx_t.shape[1]
    KD = DM // P
    DR = dt_w_t.shape[0]
    NS = a_log.shape[1]
    S = router_t.shape[1]
    R = u_w.shape[1] // S
    AD = attr_t.shape[0]
    TAPS = conv_w.shape[1]
    BROW = 32
    NB = NS // Q
    assert L == E == Q * P and NB == 4 and S * R == Q * P and TAPS == 4

    STAGES = range(-2, B + 1)

    def project_in(st):
        return 0 <= st + 2 < B

    def prepare_in(st):
        return 0 <= st + 1 < B

    def scan_in(st):
        return 0 <= st < B

    def ffn_in(st):
        return 0 <= st - 1 < B

    def turn_kinds(st):
        return ["h"] * ffn_in(st) + ["du"] * prepare_in(st) + ["hug"] * ffn_in(st) + ["z"] * scan_in(st)

    def turns_before(st):
        return sum(prepare_in(s) + Q * len(turn_kinds(s)) for s in STAGES if s < st)

    def turn(st, j, kind):
        if kind == "c":
            return turns_before(st)
        return turns_before(st) + 1 * prepare_in(st) + turn_kinds(st).index(kind) + len(turn_kinds(st)) * j

    with ExitStack() as ctx:
        def sb(name, shape, dt=F32):
            return ctx.enter_context(nc.sbuf_tensor(name, shape, dt))

        def psum(name, shape):
            return ctx.enter_context(nc.psum_tensor(name, shape, F32))

        def sem(name):
            return ctx.enter_context(nc.semaphore(name))

        ident = sb("ident", [P, P])
        iota_i = sb("iota_i", [P, S], I32)
        iota_f = sb("iota_f", [P, S])
        eps_c = sb("eps_c", [P, 1])
        minus_half = sb("minus_half", [P, 1])
        a_neg = sb("a_neg", [P, Q, NS])
        cw = sb("cw", [P, Q, TAPS])
        cb = sb("cb", [P, Q])
        dsk = sb("dsk", [P, Q])
        w_small = sb("w_small", [P, Q, BROW + NS])
        w_c = sb("w_c", [P, Q, NS])
        w_in = sb("w_in", [P, KD, P])
        w_dt = sb("w_dt", [DR + 1, P])
        router = sb("router", [P, Q, S])
        u_sb = sb("u_sb", [P, Q, S * R])
        v_sb = sb("v_sb", [P, Q, E])
        at_sb = sb("at_sb", [AD, S])
        wa_sb = sb("wa_sb", [AD, 1])
        wa_wide = sb("wa_wide", [AD, P])
        aw = sb("aw", [P, S])
        gx = sb("gx", [P, 1])
        gf = sb("gf", [P, 1])
        xs = sb("xs", [P, 3, Q, L])
        cx = sb("cx", [P, 2, KD, L])
        v = sb("v", [P, L])
        th = sb("th", [P, L])
        u = sb("u", [P, Q, L])
        xd = sb("xd", [DR + 1, L])
        xb = sb("xb", [BROW + NS, L])
        c_t = sb("c_t", [P, 2, Q, NS])
        sp = sb("sp", [P, L])
        delta = sb("delta", [P, 2, Q, L])
        du = sb("du", [P, 2, Q, L])
        dut = sb("dut", [P, L])
        zst = sb("zst", [P, 6])
        zmv = sb("zmv", [P, 2])
        zr = sb("zr", [P, 4])
        zh = sb("zh", [P, L])
        zt = sb("zt", [P, L])
        sz_t = sb("sz_t", [P, 2, Q, E])
        bbc = sb("bbc", [P, 4, L])
        dbu = sb("dbu", [P, 2, Q, L])
        state = sb("state", [P, 2, Q, L])
        acc = sb("acc", [P, 3, Q, E])
        fm = sb("fm", [P, E])
        x2 = sb("x2", [P, E])
        fst = sb("fst", [P, 6])
        fmv = sb("fmv", [P, 2])
        fr = sb("fr", [P, 3])
        h = sb("h", [P, E])
        h_t = sb("h_t", [P, Q, P])
        sc = sb("sc", [P, S])
        top = sb("top", [P, 8])
        top_i = sb("top_i", [P, 8], U32)
        top_f = sb("top_f", [P, 2])
        nmx = sb("nmx", [P, 1])
        ex = sb("ex", [P, S])
        z_sum = sb("z_sum", [P, 1])
        e1 = sb("e1", [P, S])
        e2 = sb("e2", [P, S])
        em = sb("em", [P, S])
        ga = sb("ga", [P, 8])
        gsc = sb("gsc", [P, S])
        gw = sb("gw", [P, S])
        hug = sb("hug", [P, S, R])
        hug_t = sb("hug_t", [P, Q, P])
        ot = sb("ot", [P, E])
        b_rows = nc.dram_tensor("b_rows", [B * NS, L], F32).ap()

        p_da = psum("p_da", [P, 2, L])
        p_st = psum("p_st", [P, 2, E])
        p_in = psum("p_in", [P, L])
        p_dl = psum("p_dl", [P, L])
        p_tr = psum("p_tr", [P, Q, P])
        p_f = psum("p_f", [P, E])

        s_w = sem("weights_loaded")
        s_x = [sem(f"x_loaded{i}") for i in range(3)]
        s_cx = [sem(f"ctx_loaded{i}") for i in range(2)]
        s_win = sem("w_in_loaded")
        s_wdt = sem("w_dt_loaded")
        s_bst = sem("b_stored")
        s_bbc = [sem(f"b_broadcast{i}") for i in range(4)]
        s_out = sem("out_stored")
        po_c = sem("pool_constants")
        ve_c = sem("dve_constants")
        stood = sem("stood")
        ac_c = sem("act_constants")
        pe_c = sem("pe_constants")
        pe_in = sem("pe_in_projected")
        pe_xd = sem("pe_small_projected")
        pe_dl = sem("pe_dt_projected")
        pe_turn = sem("pe_turned")
        pe_st = sem("pe_states_turned")
        pe_sc = sem("pe_scores")
        pe_hu = sem("pe_hu")
        pe_v = sem("pe_v")
        ac_v = sem("act_conv_started")
        ac_th = sem("act_tanh_v")
        ac_xd = sem("act_small_copied")
        ac_sp = sem("act_softplus")
        ac_du = sem("act_d_u")
        ac_z = sem("act_z")
        ac_turn = sem("act_turn_copied")
        ac_da = sem("act_decay")
        ac_h = sem("act_h")
        ac_sc = sem("act_scores_copied")
        ac_e = sem("act_exp_scores")
        ve_tap = sem("dve_taps")
        ve_u = sem("dve_u")
        ve_dl = sem("dve_delta")
        ve_zs = sem("dve_z_statistics")
        ve_z = sem("dve_z")
        ve_scan = sem("dve_scanned")
        ve_acc = sem("dve_accumulated")
        ve_f = sem("dve_residual_statistics")
        ve_top = sem("dve_top")
        ve_g = sem("dve_gates")
        ve_hug = sem("dve_gated")
        ve_out = sem("dve_out")
        po_dbu = sem("pool_dbu")
        po_du = sem("pool_du")
        po_f = sem("pool_f_scale")
        po_z = sem("pool_z_scale")

        N_W = 14

        block = ctx.enter_context(nc.Block())

        def started(eng, sems):
            for s in sems:
                eng.sem_inc(s, START)

        @block.sync
        def _(eng):
            def load_x(b):
                eng.dma_start(xs[:, b % 3], x[b].rearrange("(c p) l -> p c l", p=P)).then_inc(s_x[b % 3], 16)

            def load_ctx(b):
                eng.dma_start(cx[:, b % 2], ctx_t[b].rearrange("(k p) l -> p k l", p=P)).then_inc(s_cx[b % 2], 16)

            load_ctx(0)
            eng.dma_start(cw[:, :, :], conv_w.rearrange("(c p) k -> p c k", p=P)).then_inc(s_w, 16)
            eng.dma_start(w_c[:, :, :], x_w_t.rearrange("(c p) k -> p c k", p=P)[:, :, DR + NS:]).then_inc(s_w, 16)
            eng.dma_start(a_neg[:, :, :], a_log.rearrange("(c p) n -> p c n", p=P)).then_inc(s_w, 16)
            eng.dma_start(router[:, :, :], router_t.rearrange("(c p) s -> p c s", p=P)).then_inc(s_w, 16)
            eng.dma_start(at_sb[:, :], attr_t).then_inc(s_w, 16)
            with nc.allow_non_contiguous_dma(reason="one number for each channel"):
                eng.dma_start(cb[:, :], conv_b.rearrange("(c p) -> p c", p=P)).then_inc(s_w, 16)
                eng.dma_start(dsk[:, :], d_skip.rearrange("(c p) -> p c", p=P)).then_inc(s_w, 16)
                eng.dma_start(wa_sb[:, :], attr_w.rearrange("a k -> k a")).then_inc(s_w, 16)
                eng.dma_start(gx[:, :], g_xattn.partition_broadcast(P)).then_inc(s_w, 16)
                eng.dma_start(gf[:, :], g_ffn.partition_broadcast(P)).then_inc(s_w, 16)
            eng.wait_ge(po_c, 1)
            eng.dma_start(w_small[:, :, 0:DR], x_w_t.rearrange("(c p) k -> p c k", p=P)[:, :, 0:DR]).then_inc(s_w, 16)
            eng.dma_start(w_small[:, :, BROW:BROW + NS],
                          x_w_t.rearrange("(c p) k -> p c k", p=P)[:, :, DR:DR + NS]).then_inc(s_w, 16)
            load_x(0)
            load_ctx(1)
            eng.dma_start(u_sb[:, :, :], u_w.rearrange("(c p) n -> p c n", p=P)).then_inc(s_w, 16)
            eng.dma_start(v_sb[:, :, :], v_w.rearrange("(c p) n -> p c n", p=P)).then_inc(s_w, 16)
            load_x(1)
            load_x(2)

            in_blocks = in_w_t.rearrange("(k p) e -> p k e", p=P)
            dt_bias = dt_b.rearrange("(a e) -> a e", a=1)
            for st in STAGES:
                if prepare_in(st):
                    b = st + 1
                    eng.wait_ge(ac_xd, START + 2 * b + 2)
                    eng.dma_start(b_rows[b * NS:(b + 1) * NS, :], xb[BROW:BROW + NS, :]).then_inc(s_bst, 16)
                if project_in(st) and st + 2 >= 2:
                    eng.wait_ge(pe_in, START + Q * (st + 1))
                    load_ctx(st + 2)
                if 3 <= st + 1 < B:
                    eng.wait_ge(ve_f, START + 4 * Q * (st - 1))
                    load_x(st + 1)
                if scan_in(st):
                    eng.wait_ge(s_bst, 16 * (st + 1))
                if not (prepare_in(st) or project_in(st) or scan_in(st)):
                    continue
                with eng.Fori(0, Q) as j:
                    if project_in(st):
                        q = j + Q * (st + 2)
                        eng.wait_ge(pe_in, q + START)
                        eng.dma_start(w_in[:, :, :], in_blocks[:, :, bass.ds(j * P, P)]).then_inc(s_win, 16)
                    if prepare_in(st):
                        q = j + Q * (st + 1)
                        eng.wait_ge(pe_dl, q + START)
                        eng.dma_start(w_dt[0:DR, :], dt_w_t[:, bass.ds(j * P, P)]).then_inc(s_wdt, 16)
                        eng.dma_start(w_dt[DR:DR + 1, :], dt_bias[:, bass.ds(j * P, P)]).then_inc(s_wdt, 16)
                    if scan_in(st):
                        for i in range(NB):
                            n = j * NB + NS * st + i
                            eng.wait_ge(po_dbu, n - 3 + START)
                            row = b_rows[bass.ds(n, 1), :].rearrange("a l -> (a l)")
                            eng.dma_start(bbc[:, i, :], row.partition_broadcast(P)).then_inc(s_bbc[i], 16)

        @block.gpsimd
        def _(eng):
            started(eng, [po_dbu, po_du, po_f, po_z])
            eng.memset(w_small[:, :, :], 0.0).then_inc(po_c, 1)
            eng.memset(ident[:, :], 0.0).then_inc(po_c, 1)
            eng.memset(xd[:, :], 1.0).then_inc(po_c, 1)
            eng.memset(eps_c[:, :], EPS).then_inc(po_c, 1)
            eng.memset(minus_half[:, :], -0.5).then_inc(po_c, 1)
            eng.iota(iota_i[:, :], [[1, S]], base=0, channel_multiplier=0).then_inc(po_c, 1)
            eng.wait_ge(po_c, 6)
            eng.affine_select(out=ident[:, :], in_=ident[:, :], compare_op=ALU.not_equal, fill=1.0, base=0,
                              pattern=[[-1, P]], channel_multiplier=1).then_inc(po_c, 1)

            def times_b(st, j, i):
                b, n = st, j * NB + NS * st + i
                eng.wait_ge(s_bbc[i], (j + (Q * b + 1)) * 16)
                eng.wait_ge(ve_scan, (n - 1) * Q + START)
                eng.tensor_tensor(dbu[:, i % 2, :, :], du[:, b % 2, :, :],
                                  bbc[:, i:i + 1, :].to_broadcast([P, Q, L]), ALU.mult).then_inc(po_dbu, 1)

            def scale_of_f(st, j):
                f = j + Q * (st - 1)
                eng.wait_ge(ve_f, f * 4 + (START + 4))
                eng.wait_ge(ac_h, f + START)
                eng.tensor_tensor(fr[:, 0:1], fmv[:, 1:2], eps_c[:, :], ALU.add).then_inc(po_f, 1)
                eng.wait_ge(po_f, f * 3 + (START + 1))
                eng.tensor_tensor(fr[:, 1:2], fr[:, 0:1], minus_half[:, :], ALU.pow).then_inc(po_f, 1)
                eng.wait_ge(po_f, f * 3 + (START + 2))
                eng.sem_inc(stood, 1)
                eng.tensor_scalar(fr[:, 2:3], fmv[:, 0:1], fr[:, 1:2], -1.0, ALU.mult, ALU.mult).then_inc(po_f, 1)

            def scale_of_z(st, j):
                q = j + Q * st
                eng.wait_ge(ve_zs, q * 2 + (START + 2))
                eng.wait_ge(ac_z, q * 2 + START)
                eng.tensor_tensor(zr[:, 0:1], zmv[:, 1:2], eps_c[:, :], ALU.add).then_inc(po_z, 1)
                eng.wait_ge(po_z, q * 4 + (START + 1))
                eng.tensor_tensor(zr[:, 1:2], zr[:, 0:1], minus_half[:, :], ALU.pow).then_inc(po_z, 1)
                eng.wait_ge(po_z, q * 4 + (START + 2))
                eng.sem_inc(stood, 1)
                eng.tensor_scalar(zr[:, 2:3], zr[:, 1:2], 0.5, None, ALU.mult).then_inc(po_z, 1)
                eng.wait_ge(po_z, q * 4 + (START + 3))
                eng.sem_inc(stood, 1)
                eng.tensor_scalar(zr[:, 3:4], zmv[:, 0:1], zr[:, 2:3], -1.0, ALU.mult, ALU.mult).then_inc(po_z, 1)

            def times_u(st, j):
                b, q = st + 1, j + Q * (st + 1)
                eng.wait_ge(ve_dl, q + (START + 1))
                eng.wait_ge(ve_u, q + (START + 1))
                if b >= 2:
                    eng.wait_ge(po_dbu, NS * (b - 1) + START)
                eng.tensor_tensor(du[:, b % 2, bass.ds(j, 1), :], delta[:, b % 2, bass.ds(j, 1), :],
                                  u[:, bass.ds(j, 1), :], ALU.mult).then_inc(po_du, 1)

            for st in STAGES:
                if not (prepare_in(st) or ffn_in(st) or scan_in(st)):
                    continue
                if scan_in(st):
                    eng.wait_ge(po_du, START + Q * (st + 1))
                with eng.Fori(0, Q) as j:
                    if scan_in(st):
                        times_b(st, j, 0)
                        times_b(st, j, 1)
                    if ffn_in(st):
                        scale_of_f(st, j)
                    if scan_in(st):
                        scale_of_z(st, j)
                        times_b(st, j, 2)
                        times_b(st, j, 3)
                    if prepare_in(st):
                        times_u(st, j)

        @block.tensor
        def _(eng):
            started(eng, [pe_in, pe_xd, pe_dl, pe_turn, pe_st, pe_sc, pe_hu, pe_v])
            eng.wait_ge(po_c, 7)
            eng.wait_ge(s_w, 16 * N_W)
            eng.wait_ge(ve_c, 1)
            eng.matmul(p_f[:, 0:S], wa_wide[:, :], at_sb[:, :], start=True, stop=True).then_inc(pe_c, 1)
            eng.wait_ge(ac_c, 4)

            def in_projection(st, j):
                b, q = st + 2, j + Q * (st + 2)
                eng.wait_ge(s_cx[b % 2], 16 * (b // 2 + 1))
                eng.wait_ge(s_win, (q + 1) * 16)
                eng.wait_ge(ve_tap, q * 3 + START)
                for k in range(KD):
                    mm = eng.matmul(p_in[:, :], w_in[:, k, :], cx[:, b % 2, k, :], start=(k == 0), stop=(k == KD - 1))
                mm.then_inc(pe_in, 1)

            def small_projection(st):
                b = st + 1
                eng.wait_ge(ve_u, START + Q * (b + 1))
                eng.wait_ge(ve_dl, START + Q * b)
                for k in range(Q):
                    mm = eng.matmul(p_dl[0:BROW + NS, :], w_small[:, k, :], u[:, k, :], start=(k == 0), stop=(k == Q - 1))
                mm.then_inc(pe_xd, 1)
                if turn(st, 0, "c"):
                    eng.wait_ge(ac_turn, START + turn(st, 0, "c"))
                for t in range(Q):
                    for k in range(Q):
                        mm = eng.matmul(p_tr[:, 0, t * NS:(t + 1) * NS], u[:, k, t * P:(t + 1) * P], w_c[:, k, :],
                                        start=(k == 0), stop=(k == Q - 1))
                mm.then_inc(pe_turn, 1)

            def dt_projection(st, j):
                b, q = st + 1, j + Q * (st + 1)
                eng.wait_ge(s_wdt, (q + 1) * 32)
                eng.wait_ge(ac_xd, START + 2 * (b + 1))
                eng.wait_ge(ve_dl, q + START)
                eng.matmul(p_dl[:, :], w_dt[:, :], xd[:, :], start=True, stop=True).then_inc(pe_dl, 1)

            def turn_four(source, st, j, kind):
                eng.wait_ge(ac_turn, turn(st, j, kind) + START)
                for k in range(Q):
                    mm = eng.transpose(p_tr[:, k, :], source[:, k * P:(k + 1) * P], ident[:, :])
                mm.then_inc(pe_turn, 1)

            def turn_states(st, j, i):
                n = j * NB + NS * st + i
                for t in range(Q):
                    if t == 0:
                        eng.wait_ge(ve_scan, n * Q + (START + Q))
                    eng.wait_ge(ve_acc, n * Q + (START + t - 1))
                    for k in range(Q):
                        mm = eng.transpose(p_st[:, t % 2, k * P:(k + 1) * P], state[:, i % 2, k, t * P:(t + 1) * P],
                                           ident[:, :])
                    mm.then_inc(pe_st, 1)

            def scores_and_hu(st, j):
                f = j + Q * (st - 1)
                eng.wait_ge(ac_turn, turn(st, j, "h") + (START + 1))
                eng.wait_ge(ve_out, f + START)
                for k in range(Q):
                    mm = eng.matmul(p_f[:, 0:S], h_t[:, k, :], router[:, k, :], start=(k == 0), stop=(k == Q - 1))
                mm.then_inc(pe_sc, 1)
                eng.wait_ge(ac_sc, f + (START + 1))
                for k in range(Q):
                    mm = eng.matmul(p_f[:, :], h_t[:, k, :], u_sb[:, k, :], start=(k == 0), stop=(k == Q - 1))
                mm.then_inc(pe_hu, 1)

            def times_v(st, j):
                f = j + Q * (st - 1)
                eng.wait_ge(ac_turn, turn(st, j, "hug") + (START + 1))
                for k in range(Q):
                    mm = eng.matmul(p_f[:, :], hug_t[:, k, :], v_sb[:, k, :], start=(k == 0), stop=(k == Q - 1))
                mm.then_inc(pe_v, 1)

            for st in STAGES:
                if prepare_in(st):
                    small_projection(st)
                with eng.Fori(0, Q) as j:
                    if project_in(st):
                        in_projection(st, j)
                    if prepare_in(st):
                        dt_projection(st, j)
                    if scan_in(st):
                        turn_states(st, j, 0)
                    if ffn_in(st):
                        eng.wait_ge(ac_h, (j + Q * (st - 1)) + (START + 1))
                        turn_four(h, st, j, "h")
                        scores_and_hu(st, j)
                    if scan_in(st):
                        turn_states(st, j, 1)
                    if prepare_in(st):
                        eng.wait_ge(ac_du, (j + Q * (st + 1)) + (START + 1))
                        turn_four(dut, st, j, "du")
                    if scan_in(st):
                        turn_states(st, j, 2)
                    if ffn_in(st):
                        eng.wait_ge(ve_hug, (j + Q * (st - 1)) + (START + 1))
                        turn_four(hug[:, :, :].rearrange("p s r -> p (s r)"), st, j, "hug")
                        times_v(st, j)
                    if scan_in(st):
                        eng.wait_ge(ve_z, (j + Q * st) + (START + 1))
                        turn_four(zh, st, j, "z")
                        turn_states(st, j, 3)

        @block.scalar
        def _(eng):
            started(eng, [ac_v, ac_th, ac_xd, ac_sp, ac_du, ac_z, ac_turn, ac_da, ac_h, ac_sc, ac_e, s_out])
            eng.wait_ge(s_w, 16 * N_W)
            eng.activation(gx[:, :], gx[:, :], ACT.Tanh).then_inc(ac_c, 1)
            eng.activation(gf[:, :], gf[:, :], ACT.Tanh).then_inc(ac_c, 1)
            eng.activation(a_neg[:, :, :], a_neg[:, :, :], ACT.Exp).then_inc(ac_c, 1)
            eng.wait_ge(pe_c, 1)
            eng.activation(aw[:, :], p_f[:, 0:S], ACT.Exp, scale=-1.0).then_inc(ac_c, 1)
            eng.wait_ge(ve_c, 6)

            def conv_first(st, j):
                q = j + Q * (st + 2)
                eng.wait_ge(pe_in, q + (START + 1))
                eng.wait_ge(ve_u, q + START)
                eng.activation(v[:, :], p_in[:, :], ACT.Identity, bias=cb[:, bass.ds(j, 1)],
                               scale=cw[:, bass.ds(j, 1), TAPS - 1:TAPS].rearrange("p a b -> p (a b)")).then_inc(ac_v, 1)

            def tanh_v(st, j):
                q = j + Q * (st + 2)
                eng.wait_ge(ve_tap, q * 3 + (START + 3))
                eng.activation(th[:, :], v[:, :], ACT.Tanh).then_inc(ac_th, 1)

            def copy_small(st):
                b = st + 1
                eng.wait_ge(pe_xd, START + b + 1)
                eng.wait_ge(pe_dl, START + Q * b)
                eng.activation(xd[0:DR, :], p_dl[0:DR, :], ACT.Copy).then_inc(ac_xd, 1)
                if b:
                    eng.wait_ge(s_bst, 16 * b)
                eng.activation(xb[BROW:BROW + NS, :], p_dl[BROW:BROW + NS, :], ACT.Copy).then_inc(ac_xd, 1)
                eng.wait_ge(pe_turn, START + turn(st, 0, "c") + 1)
                if b >= 2:
                    eng.wait_ge(ve_acc, START + Q * NS * (b - 1))
                eng.activation(c_t[:, b % 2, :, :].rearrange("p t n -> p (t n)"), p_tr[:, 0, 0:Q * NS],
                               ACT.Copy).then_inc(ac_turn, 1)

            def softplus_tail(st, j, part):
                q = j + Q * (st + 1)
                if part == 0:
                    eng.wait_ge(pe_dl, q + (START + 1))
                    eng.wait_ge(ve_dl, q + START)
                    eng.activation(sp[:, :], p_dl[:, :], ACT.Abs).then_inc(ac_sp, 1)
                    eng.wait_ge(ac_sp, q * 3 + (START + 1))
                    eng.activation(sp[:, :], sp[:, :], ACT.Exp, scale=-1.0).then_inc(ac_sp, 1)
                else:
                    eng.wait_ge(ac_sp, q * 3 + (START + 2))
                    eng.activation(sp[:, :], sp[:, :], ACT.Ln, bias=1.0).then_inc(ac_sp, 1)

            def skip(st, j):
                q = j + Q * (st + 1)
                eng.wait_ge(ve_u, q + (START + 1))
                eng.activation(dut[:, :], u[:, bass.ds(j, 1), :].rearrange("p a l -> p (a l)"), ACT.Copy,
                               scale=dsk[:, bass.ds(j, 1)]).then_inc(ac_du, 1)

            def z_half(st, j, part):
                b, q = st, j + Q * st
                if part == 0:
                    eng.wait_ge(s_x[b % 3], 16 * (b // 3 + 1))
                    eng.wait_ge(po_z, q * 4 + (START + 4))
                    eng.wait_ge(ve_z, q + START)
                row = xs[:, b % 3, bass.ds(j, 1), :].rearrange("p a l -> p (a l)")
                eng.activation((zh, zt)[part][:, :], row, (ACT.Identity, ACT.Tanh)[part],
                               bias=zr[:, 3:4], scale=zr[:, 2:3]).then_inc(ac_z, 1)

            def copy_turn(dest, st, j, kind):
                eng.wait_ge(pe_turn, turn(st, j, kind) + (START + 1))
                eng.activation(dest, p_tr[:, :, :], ACT.Copy).then_inc(ac_turn, 1)

            def decay(st, j, i, k):
                b, tile = st, (j * NB + NS * st + i) * Q + k
                eng.wait_ge(ve_scan, tile + (START - 1))
                eng.activation(p_da[:, k % 2, :], delta[:, b % 2, k, :], ACT.Exp,
                               scale=a_neg[:, k, bass.ds(j * NB + i, 1)]).then_inc(ac_da, 1)

            def normed(st, j):
                f = j + Q * (st - 1)
                eng.wait_ge(po_f, f * 3 + (START + 3))
                eng.activation(h[:, :], x2[:, :], ACT.Identity, bias=fr[:, 2:3], scale=fr[:, 1:2]).then_inc(ac_h, 1)

            def copy_scores(st, j):
                f = j + Q * (st - 1)
                eng.wait_ge(pe_sc, f + (START + 1))
                eng.wait_ge(ve_g, f * 9 + START)
                eng.activation(sc[:, :], p_f[:, 0:S], ACT.Copy).then_inc(ac_sc, 1)

            def exp_scores(st, j):
                f = j + Q * (st - 1)
                eng.wait_ge(ve_top, f * 4 + (START + 2))
                eng.activation(ex[:, :], sc[:, :], ACT.Exp, bias=nmx[:, :], accum_out=z_sum[:, :]).then_inc(ac_e, 1)

            def store(st, j):
                f = j + Q * (st - 1)
                eng.wait_ge(ve_out, f + (START + 1))
                eng.dma_start(out[st - 1][bass.ds(j * P, P), :], ot[:, :]).then_inc(s_out, 16)

            for st in STAGES:
                if prepare_in(st):
                    copy_small(st)
                if scan_in(st):
                    eng.wait_ge(ve_dl, START + Q * (st + 1))
                with eng.Fori(0, Q) as j:
                    def decays(i, *ks):
                        if scan_in(st):
                            for k in ks:
                                decay(st, j, i, k)

                    decays(0, 0)
                    if project_in(st):
                        conv_first(st, j)
                    decays(0, 1)
                    if prepare_in(st):
                        skip(st, j)
                    decays(0, 2)
                    if prepare_in(st):
                        softplus_tail(st, j, 0)
                    decays(0, 3)
                    if prepare_in(st):
                        softplus_tail(st, j, 1)
                    if ffn_in(st):
                        normed(st, j)
                    decays(1, 0)
                    if scan_in(st):
                        z_half(st, j, 0)
                    decays(1, 1)
                    if scan_in(st):
                        z_half(st, j, 1)
                    decays(1, 2)
                    if ffn_in(st):
                        eng.wait_ge(pe_hu, (j + Q * (st - 1)) + START)
                        copy_turn(h_t[:, :, :], st, j, "h")
                    decays(1, 3)
                    if ffn_in(st):
                        copy_scores(st, j)
                    decays(2, 0)
                    if ffn_in(st):
                        exp_scores(st, j)
                    decays(2, 1)
                    if project_in(st):
                        tanh_v(st, j)
                    decays(2, 2)
                    if prepare_in(st):
                        b = st + 1
                        if b >= 3:
                            eng.wait_ge(ve_f, START + 4 * Q * (b - 2))
                        copy_turn(acc[:, b % 3, :, bass.ds(j * P, P)], st, j, "du")
                    decays(2, 3)
                    decays(3, 0, 1, 2)
                    if ffn_in(st):
                        eng.wait_ge(pe_v, (j + Q * (st - 1)) + START)
                        copy_turn(hug_t[:, :, :], st, j, "hug")
                    decays(3, 3)
                    if scan_in(st):
                        if st >= 2:
                            eng.wait_ge(ve_f, START + 4 * Q * (st - 1))
                        copy_turn(sz_t[:, st % 2, :, bass.ds(j * P, P)], st, j, "z")
                    if ffn_in(st):
                        store(st, j)
            eng.wait_ge(s_out, START + 16 * Q * B)

        @block.vector
        def _(eng):
            started(eng, [ve_tap, ve_u, ve_dl, ve_zs, ve_z, ve_scan, ve_acc, ve_f, ve_top, ve_g, ve_hug, ve_out])
            eng.wait_ge(s_w, 16 * N_W)
            eng.wait_ge(po_c, 7)
            eng.tensor_copy(wa_wide[:, :], wa_sb[:, :].to_broadcast([AD, P])).then_inc(ve_c, 1)
            eng.tensor_scalar(cw[:, :, :], cw[:, :, :], 0.5, None, ALU.mult).then_inc(ve_c, 1)
            eng.tensor_scalar(cb[:, :], cb[:, :], 0.5, None, ALU.mult).then_inc(ve_c, 1)
            eng.tensor_copy(iota_f[:, :], iota_i[:, :]).then_inc(ve_c, 1)
            eng.wait_ge(ac_c, 4)
            eng.tensor_scalar(a_neg[:, :, :], a_neg[:, :, :], -1.0, None, ALU.mult).then_inc(ve_c, 1)
            eng.tensor_scalar(aw[:, :], aw[:, :], 1.0, None, ALU.add).then_inc(ve_c, 1)
            eng.wait_ge(ve_c, 6)
            eng.reciprocal(aw[:, :], aw[:, :]).then_inc(ve_c, 1)
            eng.wait_ge(ve_c, 7)

            def taps(st, j):
                q = j + Q * (st + 2)
                eng.wait_ge(ac_v, q + (START + 1))
                for s in range(1, TAPS):
                    if s > 1:
                        eng.wait_ge(ve_tap, q * 3 + (START + s - 1))
                    eng.scalar_tensor_tensor(
                        out=v[:, s:], in0=p_in[:, 0:L - s], in1=v[:, s:], op0=ALU.mult, op1=ALU.add,
                        scalar=cw[:, bass.ds(j, 1), TAPS - 1 - s:TAPS - s].rearrange("p a b -> p (a b)"),
                    ).then_inc(ve_tap, 1)

            def silu_u(st, j):
                b, q = st + 2, j + Q * (st + 2)
                eng.wait_ge(ac_th, q + (START + 1))
                if b:
                    eng.wait_ge(pe_turn, START + turn(b - 2, 0, "c") + 1)
                    eng.wait_ge(po_du, q + (START - Q + 1))
                    eng.wait_ge(ac_du, q + (START - Q + 1))
                eng.scalar_tensor_tensor(out=u[:, bass.ds(j, 1), :].rearrange("p a l -> p (a l)"), in0=th[:, :],
                                         scalar=1.0, in1=v[:, :], op0=ALU.add, op1=ALU.mult).then_inc(ve_u, 1)

            def softplus(st, j):
                b, q = st + 1, j + Q * (st + 1)
                eng.wait_ge(ac_sp, q * 3 + (START + 3))
                if b >= 2:
                    eng.wait_ge(ac_da, START + Q * NS * (b - 1))
                    eng.wait_ge(po_du, START + Q * (b - 1))
                eng.scalar_tensor_tensor(out=delta[:, b % 2, bass.ds(j, 1), :].rearrange("p a l -> p (a l)"),
                                         in0=p_dl[:, :], scalar=0.0, in1=sp[:, :], op0=ALU.max,
                                         op1=ALU.add).then_inc(ve_dl, 1)

            def z_statistics(st, j):
                b, q = st, j + Q * st
                eng.wait_ge(s_x[b % 3], 16 * (b // 3 + 1))
                eng.wait_ge(ve_zs, q * 2 + START)
                eng.bn_stats(zst[:, :], xs[:, b % 3, bass.ds(j, 1), :].rearrange("p a l -> p (a l)")).then_inc(ve_zs, 1)
                eng.wait_ge(ve_zs, q * 2 + (START + 1))
                eng.wait_ge(po_z, q * 4 + START)
                eng.sem_inc(stood, 1)
                eng.bn_aggr(zmv[:, :], zst[:, :]).then_inc(ve_zs, 1)

            def silu_z(st, j):
                q = j + Q * st
                eng.wait_ge(ac_z, q * 2 + (START + 2))
                eng.scalar_tensor_tensor(out=zh[:, :], in0=zt[:, :], scalar=1.0, in1=zh[:, :], op0=ALU.add,
                                         op1=ALU.mult).then_inc(ve_z, 1)

            def scan(st, j, i, k):
                n = j * NB + NS * st + i
                if k == 0:
                    eng.wait_ge(po_dbu, n + (START + 1))
                    eng.wait_ge(pe_st, (n - 1) * Q + START)
                eng.wait_ge(ac_da, n * Q + (START + k + 1))
                eng.tensor_tensor_scan(state[:, i % 2, k, :], p_da[:, k % 2, :], dbu[:, i % 2, k, :], 0.0,
                                       ALU.mult, ALU.add).then_inc(ve_scan, 1)

            def accumulate(st, j, i, t):
                b, n = st, j * NB + NS * st + i
                eng.wait_ge(pe_st, n * Q + (START + t + 1))
                eng.wait_ge(ve_acc, n * Q + (START + t - Q + 1))
                eng.scalar_tensor_tensor(out=acc[:, b % 3, t, :], in0=p_st[:, t % 2, :],
                                         scalar=c_t[:, b % 2, t, bass.ds(j * NB + i, 1)], in1=acc[:, b % 3, t, :],
                                         op0=ALU.mult, op1=ALU.add).then_inc(ve_acc, 1)

            def residual(st, j):
                b, f = st - 1, j + Q * (st - 1)
                block_b = lambda t, depth: t[:, b % depth, bass.ds(j, 1), :].rearrange("p a l -> p (a l)")
                eng.wait_ge(ve_f, f * 4 + START)
                eng.tensor_tensor(fm[:, :], block_b(acc, 3), block_b(sz_t, 2), ALU.mult).then_inc(ve_f, 1)
                eng.wait_ge(ve_f, f * 4 + (START + 1))
                eng.wait_ge(ac_h, f + START)
                eng.wait_ge(ve_out, f + START)
                eng.scalar_tensor_tensor(out=x2[:, :], in0=fm[:, :], scalar=gx[:, :],
                                         in1=xs[:, b % 3, bass.ds(j, 1), :].rearrange("p a l -> p (a l)"),
                                         op0=ALU.mult, op1=ALU.add).then_inc(ve_f, 1)
                eng.wait_ge(ve_f, f * 4 + (START + 2))
                eng.bn_stats(fst[:, :], x2[:, :]).then_inc(ve_f, 1)
                eng.wait_ge(ve_f, f * 4 + (START + 3))
                eng.wait_ge(po_f, f * 3 + START)
                eng.sem_inc(stood, 1)
                eng.bn_aggr(fmv[:, :], fst[:, :]).then_inc(ve_f, 1)

            def best_two(st, j):
                f = j + Q * (st - 1)
                eng.wait_ge(ac_sc, f + (START + 1))
                eng.wait_ge(ve_g, f * 9 + START)
                eng.sem_inc(stood, 1)
                eng.max(top[:, :], sc[:, :]).then_inc(ve_top, 1)
                eng.wait_ge(ve_top, f * 4 + (START + 1))
                eng.wait_ge(ac_e, f + START)
                eng.tensor_scalar(nmx[:, :], top[:, 0:1], -1.0, None, ALU.mult).then_inc(ve_top, 1)
                eng.max_index(top_i[:, :], top[:, :], sc[:, :]).then_inc(ve_top, 1)
                eng.wait_ge(ve_top, f * 4 + (START + 3))
                eng.tensor_copy(top_f[:, :], top_i[:, 0:2]).then_inc(ve_top, 1)

            def gates(st, j):
                f = j + Q * (st - 1)
                made = lambda n: eng.wait_ge(ve_g, f * 9 + (START + n))
                eng.wait_ge(ac_e, f + (START + 1))
                eng.wait_ge(ve_top, f * 4 + (START + 4))
                eng.wait_ge(ve_hug, f + START)
                eng.scalar_tensor_tensor(out=e1[:, :], in0=iota_f[:, :], scalar=top_f[:, 0:1], in1=ex[:, :],
                                         op0=ALU.is_equal, op1=ALU.mult).then_inc(ve_g, 1)
                eng.scalar_tensor_tensor(out=e2[:, :], in0=iota_f[:, :], scalar=top_f[:, 1:2], in1=ex[:, :],
                                         op0=ALU.is_equal, op1=ALU.mult).then_inc(ve_g, 1)
                made(2)
                eng.scalar_tensor_tensor(out=em[:, :], in0=e1[:, :], scalar=1.0, in1=e2[:, :], op0=ALU.mult,
                                         op1=ALU.add, accum_out=ga[:, 0:1]).then_inc(ve_g, 1)
                made(3)
                eng.scalar_tensor_tensor(out=ga[:, 1:2], in0=z_sum[:, :], scalar=GATE_EPS, in1=ga[:, 0:1],
                                         op0=ALU.mult, op1=ALU.add).then_inc(ve_g, 1)
                eng.scalar_tensor_tensor(out=gsc[:, :], in0=em[:, :], scalar=1.0, in1=aw[:, :], op0=ALU.mult,
                                         op1=ALU.mult, accum_out=ga[:, 3:4]).then_inc(ve_g, 1)
                made(5)
                eng.reciprocal(ga[:, 2:3], ga[:, 1:2]).then_inc(ve_g, 1)
                made(6)
                eng.tensor_scalar(ga[:, 4:5], ga[:, 3:4], ga[:, 2:3], 0.2, ALU.mult, ALU.mult).then_inc(ve_g, 1)
                made(7)
                eng.tensor_scalar(ga[:, 5:6], ga[:, 4:5], 0.9, ga[:, 2:3], ALU.add, ALU.mult).then_inc(ve_g, 1)
                made(8)
                eng.tensor_scalar(gw[:, :], em[:, :], ga[:, 5:6], gf[:, :], ALU.mult, ALU.mult).then_inc(ve_g, 1)
                made(9)
                eng.wait_ge(pe_hu, f + (START + 1))
                eng.tensor_tensor(hug[:, :, :], p_f[:, :].rearrange("p (s r) -> p s r", r=R),
                                  gw[:, :].unsqueeze(2).to_broadcast([P, S, R]), ALU.mult).then_inc(ve_hug, 1)

            def add_out(st, j):
                f = j + Q * (st - 1)
                eng.wait_ge(pe_v, f + (START + 1))
                eng.wait_ge(s_out, f * 16 + START)
                eng.tensor_tensor(ot[:, :], p_f[:, :], x2[:, :], ALU.add).then_inc(ve_out, 1)

            for st in STAGES:
                if scan_in(st) or ffn_in(st):
                    eng.wait_ge(ac_turn, START + turns_before(st))
                with eng.Fori(0, Q) as j:
                    def scans(i):
                        if scan_in(st):
                            for k in range(Q):
                                scan(st, j, i, k)
                                if i:
                                    accumulate(st, j, i - 1, k)

                    if ffn_in(st):
                        residual(st, j)
                    if scan_in(st):
                        z_statistics(st, j)
                    scans(0)
                    scans(1)
                    if project_in(st):
                        taps(st, j)
                    if ffn_in(st):
                        best_two(st, j)
                    scans(2)
                    if prepare_in(st):
                        softplus(st, j)
                    if scan_in(st):
                        silu_z(st, j)
                    if ffn_in(st):
                        gates(st, j)
                    scans(3)
                    if project_in(st):
                        silu_u(st, j)
                    if ffn_in(st):
                        add_out(st, j)
                    if scan_in(st):
                        for t in range(Q):
                            accumulate(st, j, NB - 1, t)


def kernel(**inputs):
    import numpy as _np
    import concourse.bacc as _bacc
    from concourse import mybir as _mybir
    from concourse.bass_utils import run_bass_kernel_spmd as _run

    given = {k: _np.asarray(a) for k, a in inputs.items()}
    s, hdim, r = given["L0_ffn_U"].shape
    arrays = {
        "x": given["x"],
        "ctx_t": given["ctx_1024"].transpose(0, 2, 1),
        "g_xattn": given["g_xattn"],
        "g_ffn": given["g_ffn"],
        "in_w_t": given["L0_xattn_in_proj_w"].T,
        "conv_w": given["L0_xattn_conv_w"],
        "conv_b": given["L0_xattn_conv_b"],
        "x_w_t": given["L0_xattn_x_proj_w"].T,
        "dt_w_t": given["L0_xattn_dt_proj_w"].T,
        "dt_b": given["L0_xattn_dt_proj_b"],
        "a_log": given["L0_xattn_A_log"],
        "d_skip": given["L0_xattn_D"],
        "router_t": given["L0_ffn_Wr"].T,
        "u_w": given["L0_ffn_U"].transpose(1, 0, 2).reshape(hdim, s * r),
        "v_w": given["L0_ffn_V"].reshape(s * r, hdim),
        "attr_t": given["L0_ffn_attr"].T,
        "attr_w": given["L0_ffn_Wa"],
    }
    nc = _bacc.Bacc("TRN2", target_bir_lowering=False, num_devices=1)
    maps, args = {}, []
    for name, a in arrays.items():
        a = _np.ascontiguousarray(a)
        maps[f"in_{name}"] = a
        args.append(nc.dram_tensor(f"in_{name}", a.shape, _mybir.dt.from_np(a.dtype), kind="ExternalInput").ap())
    args.append(nc.dram_tensor("out_0", given["x"].shape, _mybir.dt.float32, kind="ExternalOutput").ap())
    flamingo(nc, *args)
    got = _run(nc, [maps], core_ids=[0])
    return got.results[0]["out_0"]
```

```python
from contextlib import ExitStack, nullcontext

import concourse.bass as bass
from concourse import mybir

ALU = mybir.AluOpType
ACT = mybir.ActivationFunctionType
F32 = mybir.dt.float32
I32 = mybir.dt.int32
U32 = mybir.dt.uint32

P = 128
Q = 4
EPS = 1e-5
GATE_EPS = 1e-8
START = 16


def flamingo(nc, x, ctx_t, g_xattn, g_ffn, in_w_t, conv_w, conv_b, x_w_t, dt_w_t, dt_b, a_log, d_skip,
             router_t, u_w, v_w, attr_t, attr_w, out):
    B, L, E = x.shape
    DM = ctx_t.shape[1]
    KD = DM // P
    DR = dt_w_t.shape[0]
    NS = a_log.shape[1]
    S = router_t.shape[1]
    R = u_w.shape[1] // S
    AD = attr_t.shape[0]
    TAPS = conv_w.shape[1]
    BROW = 32
    NB = NS // Q
    assert L == E == Q * P and NB == 4 and S * R == Q * P and TAPS == 4

    RUNS = [run for st in range(B) for run in ((st, 0, 1), (st, 1, Q))] + [(B, 0, Q), (B + 1, 0, 1)]

    def project_in(st):
        return 0 <= st + 2 < B

    def prepare_in(st):
        return 0 <= st + 1 < B

    def scan_in(st):
        return 0 <= st < B

    def ffn_in(st):
        return 0 <= st - 1 < B

    def ffn_end_in(st, j0):
        return 0 <= Q * (st - 1) + j0 - 1 < Q * B

    def turn_kinds(run):
        st = run[0]
        first = prepare_in(st) and run[1] == 0
        return (["small"] * first + ["h"] * ffn_in(st) + ["du"] * prepare_in(st) + ["c"] * first
                + ["z"] * scan_in(st) + ["hug"] * ffn_in(st))

    OPENING_KINDS = ["small"] + ["du"] * Q + ["c"]

    def turns_before(run):
        return len(OPENING_KINDS) + sum((r[2] - r[1]) * len(turn_kinds(r)) for r in RUNS if r < run)

    def turn(run, j, kind):
        first = turns_before(run) + (turn_kinds(run).index(kind) if kind else 0)
        return (j - run[1]) * len(turn_kinds(run)) + first

    def each_turn(eng, run):
        return eng.Fori(run[1], run[2]) if run[2] - run[1] > 1 else nullcontext(run[1])

    with ExitStack() as ctx:
        def sb(name, shape, dt=F32):
            return ctx.enter_context(nc.sbuf_tensor(name, shape, dt))

        def psum(name, shape):
            return ctx.enter_context(nc.psum_tensor(name, shape, F32))

        def sem(name):
            return ctx.enter_context(nc.semaphore(name))

        ident = sb("ident", [P, P])
        iota_i = sb("iota_i", [P, S], I32)
        iota_f = sb("iota_f", [P, S])
        eps_c = sb("eps_c", [P, 1])
        minus_half = sb("minus_half", [P, 1])
        a_neg = sb("a_neg", [P, Q, NS])
        cw = sb("cw", [P, Q, TAPS])
        cb = sb("cb", [P, Q])
        dsk = sb("dsk", [P, Q])
        w_small = sb("w_small", [P, Q, BROW + 2 * NS])
        w_in = sb("w_in", [P, KD, P])
        w_dt = sb("w_dt", [DR + 1, P])
        router = sb("router", [P, Q, S])
        u_sb = sb("u_sb", [P, Q, S * R])
        v_sb = sb("v_sb", [P, Q, E])
        at_sb = sb("at_sb", [AD, S])
        wa_sb = sb("wa_sb", [AD, 1])
        wa_wide = sb("wa_wide", [AD, P])
        aw = sb("aw", [P, S])
        gx = sb("gx", [P, 1])
        gf = sb("gf", [P, 1])
        xs = sb("xs", [P, 3, Q, L])
        cx = sb("cx", [P, 2, KD, L])
        v = sb("v", [P, L])
        th = sb("th", [P, L])
        u = sb("u", [P, Q, L])
        xd = sb("xd", [DR + 1, L])
        bc = sb("bc", [2 * NS, L])
        c_t = sb("c_t", [P, 2, Q, NS])
        sp = sb("sp", [P, L])
        delta = sb("delta", [P, 2, Q, L])
        du = sb("du", [P, 2, Q, L])
        dut = sb("dut", [P, L])
        zst = sb("zst", [P, 6])
        zmv = sb("zmv", [P, 2])
        zr = sb("zr", [P, 4])
        zh = sb("zh", [P, L])
        zt = sb("zt", [P, L])
        sz_t = sb("sz_t", [P, 2, Q, E])
        bbc = sb("bbc", [P, 4, L])
        dbu = sb("dbu", [P, 2, Q, L])
        state = sb("state", [P, 2, Q, L])
        acc = sb("acc", [P, 3, Q, E])
        fm = sb("fm", [P, E])
        x2 = sb("x2", [P, E])
        fst = sb("fst", [P, 6])
        fmv = sb("fmv", [P, 2])
        fr = sb("fr", [P, 3])
        h = sb("h", [P, E])
        h_t = sb("h_t", [P, Q, P])
        sc = sb("sc", [P, S])
        top = sb("top", [P, 8])
        top_i = sb("top_i", [P, 8], U32)
        top_f = sb("top_f", [P, 2])
        nmx = sb("nmx", [P, 1])
        ex = sb("ex", [P, S])
        z_sum = sb("z_sum", [P, 1])
        e1 = sb("e1", [P, S])
        e2 = sb("e2", [P, S])
        em = sb("em", [P, S])
        ga = sb("ga", [P, 8])
        gsc = sb("gsc", [P, S])
        gw = sb("gw", [P, S])
        hug = sb("hug", [P, S, R])
        hug_t = sb("hug_t", [P, Q, P])
        ot = sb("ot", [P, E])
        out_rows = out.rearrange("b l e -> (b l) e")
        b_rows = nc.dram_tensor("b_rows", [B * NS, L], F32).ap()

        p_scan = psum("p_scan", [P, 5, L])
        p_da = p_scan[:, 0:3, :]
        p_st = p_scan[:, 3:5, :]
        p_pr = psum("p_pr", [P, L])
        p_tr = psum("p_tr", [P, Q, P])
        p_rows = p_tr[:, :, :].rearrange("p t m -> p (t m)")
        p_f = psum("p_f", [P, E])

        s_w = sem("weights_loaded")
        s_x = [sem(f"x_loaded{i}") for i in range(3)]
        s_cx = [sem(f"ctx_loaded{i}") for i in range(2)]
        s_first = sem("in_projection_weights_loaded")
        s_conv = sem("conv_weights_loaded")
        s_second = sem("prepare_weights_loaded")
        s_win = sem("w_in_loaded")
        s_wdt = sem("w_dt_loaded")
        s_bst = sem("b_stored")
        s_bbc = [sem(f"b_broadcast{i}") for i in range(4)]
        s_out = sem("out_stored")
        po_c = sem("pool_constants")
        ve_c = sem("dve_constants")
        stood = sem("stood")
        ac_c = sem("act_constants")
        pe_c = sem("pe_constants")
        pe_in = sem("pe_in_projected")
        pe_dl = sem("pe_dt_projected")
        pe_turn = sem("pe_turned")
        pe_st = sem("pe_states_turned")
        pe_sc = sem("pe_scores")
        pe_hu = sem("pe_hu")
        pe_x2 = sem("pe_x2")
        pe_v = sem("pe_v")
        ac_v = sem("act_conv_started")
        ac_th = sem("act_tanh_v")
        ac_xd = sem("act_small_copied")
        ac_sp = sem("act_softplus")
        ac_du = sem("act_d_u")
        ac_z = sem("act_z")
        ac_turn = sem("act_turn_copied")
        ac_da = sem("act_decay")
        ac_h = sem("act_h")
        ac_sc = sem("act_scores_copied")
        ac_e = sem("act_exp_scores")
        ac_out = sem("act_out")
        ve_tap = sem("dve_taps")
        ve_u = sem("dve_u")
        ve_dl = sem("dve_delta")
        ve_zs = sem("dve_z_statistics")
        ve_z = sem("dve_z")
        ve_scan = sem("dve_scanned")
        ve_acc = sem("dve_accumulated")
        ve_f = sem("dve_residual_statistics")
        ve_top = sem("dve_top")
        ve_g = sem("dve_gates")
        ve_hug = sem("dve_gated")
        po_dbu = sem("pool_dbu")
        po_du = sem("pool_du")
        po_f = sem("pool_f_scale")
        po_z = sem("pool_z_scale")

        w_in_all = xs[:, 2, 0:KD, :]
        w_dt_all = xs[0:DR + 1, 2, KD, :]
        v_open = [sz_t[:, 1], sz_t[:, 0]]
        th_open = [acc[:, 2], acc[:, 1]]
        dut_open = state[:, 0]
        sp_open = state[:, 1]
        banks_open = [[p_scan[:, e, :] for e in range(Q)],
                      [p_scan[:, 4, :], p_pr[:, :], p_f[:, :], p_scan[:, 4, :]]]

        DA_BANK = [m % 3 for m in range(Q * NB - 1)] + [1]
        DA_AGO = [4, 2, 4] + [3] * (Q * NB - 4) + [2]
        for m in range(Q * NB):
            assert (DA_BANK + DA_BANK)[m:m + Q * NB + 1][::-1].index(DA_BANK[m], 1) == DA_AGO[m]

        N_W = 7

        block = ctx.enter_context(nc.Block())

        def started(eng, sems):
            for s in sems:
                eng.sem_inc(s, START)

        @block.sync
        def _(eng):
            def load_x(b):
                eng.dma_start(xs[:, b % 3], x[b].rearrange("(c p) l -> p c l", p=P)).then_inc(s_x[b % 3], 16)

            def load_ctx(b):
                eng.dma_start(cx[:, b % 2], ctx_t[b].rearrange("(k p) l -> p k l", p=P)).then_inc(s_cx[b % 2], 16)

            load_ctx(0)
            eng.dma_start(w_in_all, in_w_t.rearrange("(k p) e -> p k e", p=P)).then_inc(s_first, 16)
            eng.dma_start(cw[:, :, :], conv_w.rearrange("(c p) k -> p c k", p=P)).then_inc(s_conv, 16)
            with nc.allow_non_contiguous_dma(reason="one number for each channel"):
                eng.dma_start(cb[:, :], conv_b.rearrange("(c p) -> p c", p=P)).then_inc(s_conv, 16)
                eng.dma_start(dsk[:, :], d_skip.rearrange("(c p) -> p c", p=P)).then_inc(s_second, 16)
            by_channel = x_w_t.rearrange("(c p) k -> p c k", p=P)
            eng.dma_start(w_small[:, :, 0:DR], by_channel[:, :, 0:DR]).then_inc(s_second, 16)
            eng.dma_start(w_small[:, :, BROW:], by_channel[:, :, DR:]).then_inc(s_second, 16)
            eng.dma_start(w_dt_all[0:DR, :], dt_w_t).then_inc(s_second, 16)
            eng.dma_start(w_dt_all[DR:DR + 1, :], dt_b.rearrange("(a e) -> a e", a=1)).then_inc(s_second, 16)
            eng.dma_start(a_neg[:, :, :], a_log.rearrange("(c p) n -> p c n", p=P)).then_inc(s_second, 16)
            load_ctx(1)
            load_x(0)
            eng.dma_start(router[:, :, :], router_t.rearrange("(c p) s -> p c s", p=P)).then_inc(s_w, 16)
            eng.dma_start(at_sb[:, :], attr_t).then_inc(s_w, 16)
            with nc.allow_non_contiguous_dma(reason="one number for each partition"):
                eng.dma_start(wa_sb[:, :], attr_w.rearrange("a k -> k a")).then_inc(s_w, 16)
                eng.dma_start(gx[:, :], g_xattn.partition_broadcast(P)).then_inc(s_w, 16)
                eng.dma_start(gf[:, :], g_ffn.partition_broadcast(P)).then_inc(s_w, 16)

            def store_b(b):
                first = turns_before((b - 1, 0, 1)) if b else 0
                eng.wait_ge(ac_turn, START + first + 1)
                eng.dma_start(b_rows[b * NS:(b + 1) * NS, :], bc[0:NS, :]).then_inc(s_bst, 16)

            eng.wait_ge(pe_in, START + Q)
            load_ctx(2)
            store_b(0)
            in_blocks = in_w_t.rearrange("(k p) e -> p k e", p=P)
            dt_bias = dt_b.rearrange("(a e) -> a e", a=1)
            for run in RUNS:
                st = run[0]
                if scan_in(st):
                    eng.wait_ge(s_bst, 16 * (st + 1))
                if not (prepare_in(st) or project_in(st) or scan_in(st)):
                    continue
                with each_turn(eng, run) as j:
                    if scan_in(st):
                        for i in range(NB):
                            n = j * NB + NS * st + i
                            eng.wait_ge(po_dbu, n - 3 + START)
                            row = b_rows[bass.ds(n, 1), :].rearrange("a l -> (a l)")
                            eng.dma_start(bbc[:, i, :], row.partition_broadcast(P)).then_inc(s_bbc[i], 16)
                    if project_in(st):
                        q = j + Q * (st + 2)
                        eng.wait_ge(pe_in, q + START)
                        eng.dma_start(w_in[:, :, :], in_blocks[:, :, bass.ds(j * P, P)]).then_inc(s_win, 16)
                    if prepare_in(st):
                        q = j + Q * (st + 1)
                        eng.wait_ge(pe_dl, q + START)
                        eng.dma_start(w_dt[0:DR, :], dt_w_t[:, bass.ds(j * P, P)]).then_inc(s_wdt, 16)
                        eng.dma_start(w_dt[DR:DR + 1, :], dt_bias[:, bass.ds(j * P, P)]).then_inc(s_wdt, 16)
                if run[1] > 0 or not scan_in(st):
                    continue
                if prepare_in(st):
                    store_b(st + 1)
                if st == 0:
                    eng.dma_start(u_sb[:, :, :], u_w.rearrange("(c p) n -> p c n", p=P)).then_inc(s_w, 16)
                    eng.dma_start(v_sb[:, :, :], v_w.rearrange("(c p) n -> p c n", p=P)).then_inc(s_w, 16)
                    load_x(1)
                    eng.wait_ge(pe_in, START + 2 * Q)
                    eng.wait_ge(pe_dl, START + Q)
                    load_x(2)
                if project_in(st + 1):
                    eng.wait_ge(pe_in, START + Q * (st + 2))
                    load_ctx(st + 3)
                if 3 <= st + 1 < B:
                    eng.wait_ge(ve_f, START + 4 * Q * (st - 1))
                    load_x(st + 1)

        @block.gpsimd
        def _(eng):
            started(eng, [po_dbu, po_du, po_f, po_z])
            eng.memset(w_small[:, :, DR:BROW], 0.0).then_inc(po_c, 1)
            eng.memset(ident[:, :], 0.0).then_inc(po_c, 1)
            eng.memset(xd[:, :], 1.0).then_inc(po_c, 1)
            eng.memset(eps_c[:, :], EPS).then_inc(po_c, 1)
            eng.memset(minus_half[:, :], -0.5).then_inc(po_c, 1)
            eng.iota(iota_i[:, :], [[1, S]], base=0, channel_multiplier=0).then_inc(po_c, 1)
            eng.wait_ge(po_c, 6)
            eng.affine_select(out=ident[:, :], in_=ident[:, :], compare_op=ALU.not_equal, fill=1.0, base=0,
                              pattern=[[-1, P]], channel_multiplier=1).then_inc(po_c, 1)

            def times_b(st, j, i):
                b, n = st, j * NB + NS * st + i
                eng.wait_ge(s_bbc[i], (j + (Q * b + 1)) * 16)
                eng.wait_ge(ve_scan, (n - 1) * Q + START)
                eng.tensor_tensor(dbu[:, i % 2, :, :], du[:, b % 2, :, :],
                                  bbc[:, i:i + 1, :].to_broadcast([P, Q, L]), ALU.mult).then_inc(po_dbu, 1)

            def scale_of_f(st, j):
                f = j + Q * (st - 1)
                eng.wait_ge(ve_f, f * 4 + (START + 4))
                eng.wait_ge(ac_h, f + START)
                eng.tensor_tensor(fr[:, 0:1], fmv[:, 1:2], eps_c[:, :], ALU.add).then_inc(po_f, 1)
                eng.wait_ge(po_f, f * 3 + (START + 1))
                eng.tensor_tensor(fr[:, 1:2], fr[:, 0:1], minus_half[:, :], ALU.pow).then_inc(po_f, 1)
                eng.wait_ge(po_f, f * 3 + (START + 2))
                eng.sem_inc(stood, 1)
                eng.tensor_scalar(fr[:, 2:3], fmv[:, 0:1], fr[:, 1:2], -1.0, ALU.mult, ALU.mult).then_inc(po_f, 1)

            def scale_of_z(st, j):
                q = j + Q * st
                eng.wait_ge(ve_zs, q * 2 + (START + 2))
                eng.wait_ge(ac_z, q * 2 + START)
                eng.tensor_tensor(zr[:, 0:1], zmv[:, 1:2], eps_c[:, :], ALU.add).then_inc(po_z, 1)
                eng.wait_ge(po_z, q * 4 + (START + 1))
                eng.tensor_tensor(zr[:, 1:2], zr[:, 0:1], minus_half[:, :], ALU.pow).then_inc(po_z, 1)
                eng.wait_ge(po_z, q * 4 + (START + 2))
                eng.sem_inc(stood, 1)
                eng.tensor_scalar(zr[:, 2:3], zr[:, 1:2], 0.5, None, ALU.mult).then_inc(po_z, 1)
                eng.wait_ge(po_z, q * 4 + (START + 3))
                eng.sem_inc(stood, 1)
                eng.tensor_scalar(zr[:, 3:4], zmv[:, 0:1], zr[:, 2:3], -1.0, ALU.mult, ALU.mult).then_inc(po_z, 1)

            def times_u(st, j):
                b, q = st + 1, j + Q * (st + 1)
                eng.wait_ge(ve_dl, q + (START + 1))
                eng.wait_ge(ve_u, q + (START + 1))
                if b >= 2:
                    eng.wait_ge(po_dbu, NS * (b - 1) + START)
                eng.tensor_tensor(du[:, b % 2, bass.ds(j, 1), :], delta[:, b % 2, bass.ds(j, 1), :],
                                  u[:, bass.ds(j, 1), :], ALU.mult).then_inc(po_du, 1)

            for e in range(Q):
                times_u(-1, e)
            for run in RUNS:
                st = run[0]
                if not (prepare_in(st) or ffn_in(st) or scan_in(st)):
                    continue
                if scan_in(st) and run[1] == 0:
                    eng.wait_ge(po_du, START + Q * (st + 1))
                with each_turn(eng, run) as j:
                    if scan_in(st):
                        times_b(st, j, 0)
                        if prepare_in(st) and run[1] > 0:
                            times_u(st, j - 1)
                        times_b(st, j, 1)
                    if ffn_in(st):
                        scale_of_f(st, j)
                    if scan_in(st):
                        scale_of_z(st, j)
                        times_b(st, j, 2)
                        times_b(st, j, 3)
                if prepare_in(st) and run[2] == Q:
                    times_u(st, Q - 1)

        @block.tensor
        def _(eng):
            started(eng, [pe_in, pe_dl, pe_turn, pe_st, pe_sc, pe_hu, pe_x2, pe_v])

            def in_projection(st, j, k):
                b, q = st + 2, j + Q * (st + 2)
                if k == 0:
                    eng.wait_ge(s_cx[b % 2], 16 * (b // 2 + 1))
                    eng.wait_ge(s_win, (q - 2 * Q + 1) * 16)
                    eng.wait_ge(ve_tap, q * 3 + START)
                    eng.wait_ge(ve_dl, q + (START - Q))
                mm = eng.matmul(p_pr[:, :], w_in[:, k, :], cx[:, b % 2, k, :], start=(k == 0), stop=(k == KD - 1))
                if k == KD - 1:
                    mm.then_inc(pe_in, 1)

            def in_projection_open(b, e):
                eng.wait_ge(s_cx[b], 16)
                for k in range(KD):
                    mm = eng.matmul(banks_open[b][e], w_in_all[:, k, e * P:(e + 1) * P], cx[:, b, k, :],
                                    start=(k == 0), stop=(k == KD - 1))
                mm.then_inc(pe_in, 1)

            def small_projection(b, uses):
                eng.wait_ge(ac_turn, START + uses)
                for k in range(Q):
                    eng.wait_ge(ve_u, START + Q * b + k + 1)
                    mm = eng.matmul(p_rows[0:BROW + 2 * NS, :], w_small[:, k, :], u[:, k, :], start=(k == 0), stop=(k == Q - 1))
                mm.then_inc(pe_turn, 1)

            def turn_c(uses):
                eng.wait_ge(ac_turn, START + uses)
                for t in range(Q):
                    mm = eng.transpose(p_tr[:, t, 0:2 * NS], bc[:, t * P:(t + 1) * P], ident[0:2 * NS, 0:2 * NS])
                mm.then_inc(pe_turn, 1)

            def dt_projection(st, j):
                b, q = st + 1, j + Q * (st + 1)
                eng.wait_ge(s_wdt, (q - Q + 1) * 32)
                eng.wait_ge(ac_xd, START + b + 1)
                if project_in(st):
                    eng.wait_ge(ve_tap, q * 3 + (START + 3 * Q + 3))
                else:
                    eng.wait_ge(ve_dl, q + START)
                eng.matmul(p_pr[:, :], w_dt[:, :], xd[:, :], start=True, stop=True).then_inc(pe_dl, 1)

            def turn_four(source, uses):
                eng.wait_ge(ac_turn, uses + START)
                for k in range(Q):
                    mm = eng.transpose(p_tr[:, k, :], source[:, k * P:(k + 1) * P], ident[:, :])
                mm.then_inc(pe_turn, 1)

            def turn_states(st, j, i, t):
                n = j * NB + NS * st + i
                if t == 0:
                    eng.wait_ge(ve_scan, n * Q + (START + Q))
                eng.wait_ge(ve_acc, n * Q + (START + t - 1))
                for k in range(Q):
                    mm = eng.transpose(p_st[:, t % 2, k * P:(k + 1) * P], state[:, i % 2, k, t * P:(t + 1) * P],
                                       ident[:, :])
                mm.then_inc(pe_st, 1)

            def scores(run, j):
                f = j + Q * (run[0] - 1)
                eng.wait_ge(ac_turn, turn(run, j, "h") + (START + 1))
                eng.wait_ge(ac_out, f + START)
                for k in range(Q):
                    mm = eng.matmul(p_f[:, 0:S], h_t[:, k, :], router[:, k, :], start=(k == 0), stop=(k == Q - 1))
                mm.then_inc(pe_sc, 1)

            def times_u_weights(st, j, k):
                if k == 0:
                    eng.wait_ge(ac_sc, (j + Q * (st - 1)) + (START + 1))
                mm = eng.matmul(p_f[:, :], h_t[:, k, :], u_sb[:, k, :], start=(k == 0), stop=(k == Q - 1))
                if k == Q - 1:
                    mm.then_inc(pe_hu, 1)

            def turn_gated(run, j):
                eng.wait_ge(ve_hug, (j + Q * (run[0] - 1)) + (START + 1))
                eng.matmul(p_f[:, :], ident[:, :], x2[:, :], start=True, stop=False).then_inc(pe_x2, 1)
                turn_four(hug[:, :, :].rearrange("p s r -> p (s r)"), turn(run, j, "hug"))

            def times_v(j, run):
                f = j + (Q * (run[0] - 1) - 1)
                eng.wait_ge(ac_turn, turn(run, j, None) + START)
                for k in range(Q):
                    mm = eng.matmul(p_f[:, :], hug_t[:, k, :], v_sb[:, k, :], start=False, stop=(k == Q - 1))
                mm.then_inc(pe_v, 1)

            eng.wait_ge(s_first, 16)
            for e in range(Q):
                in_projection_open(0, e)
            for e in range(Q - 1):
                in_projection_open(1, e)
            eng.wait_ge(s_second, 16 * 6)
            eng.wait_ge(po_c, 7)
            small_projection(0, 0)
            eng.wait_ge(ac_xd, START + 1)
            for e in range(Q):
                eng.wait_ge(ve_tap, START + 3 * (e + 1))
                eng.matmul(p_scan[:, e, :], w_dt_all[:, e * P:(e + 1) * P], xd[:, :], start=True, stop=True).then_inc(pe_dl, 1)
            eng.wait_ge(ve_tap, START + 3 * Q + 3)
            in_projection_open(1, 3)
            for e in range(Q):
                eng.wait_ge(ac_du, START + e + 1)
                turn_four(dut_open[:, e, :], 1 + e)
            turn_c(1 + Q)
            eng.wait_ge(s_w, 16 * 5)
            eng.wait_ge(ve_c, 3)
            eng.wait_ge(ve_tap, START + 3 * Q + 9)
            eng.matmul(p_f[:, 0:S], wa_wide[:, :], at_sb[:, :], start=True, stop=True).then_inc(pe_c, 1)

            for run in RUNS:
                st = run[0]
                if prepare_in(st) and run[1] == 0:
                    if ffn_in(st) and ffn_end_in(st, 0):
                        times_v(0, run)
                    small_projection(st + 1, turn(run, 0, "small"))
                if st == 1 and run[1] == 0:
                    eng.wait_ge(s_w, 16 * N_W)
                    eng.wait_ge(ac_c, 4)
                with each_turn(eng, run) as j:
                    after = {}
                    if ffn_end_in(st, run[1]) and not (prepare_in(st) and run[1] == 0):
                        times_v(j, run)
                    if project_in(st):
                        in_projection(st, j, 0)
                        if ffn_in(st):
                            after[0, 1] = [lambda: in_projection(st, j, 1)]
                        else:
                            in_projection(st, j, 1)
                    if ffn_in(st):
                        after[0, 3] = [lambda: eng.wait_ge(ac_h, (j + Q * (st - 1)) + (START + 1)),
                                       lambda: turn_four(h, turn(run, j, "h"))]
                        after[1, 1] = [lambda: scores(run, j)]
                        for k in range(Q):
                            after[2, k] = [lambda k=k: times_u_weights(st, j, k)]
                        after[3, 3] = [lambda: turn_gated(run, j)]
                    if prepare_in(st):
                        after.setdefault((1, 1), []).extend([
                            lambda: eng.wait_ge(ac_du, (j + Q * (st + 1)) + (START + 1)),
                            lambda: turn_four(dut, turn(run, j, "du"))])
                        after[1, 2] = [lambda: dt_projection(st, j)]
                        if run[1] == 0:
                            after[1, 3] = [lambda: turn_c(turn(run, j, "c"))]
                    if scan_in(st):
                        after.setdefault((2, 2), []).extend([
                            lambda: eng.wait_ge(ve_z, (j + Q * st) + (START + 1)),
                            lambda: turn_four(zh, turn(run, j, "z"))])
                    for i in range(NB):
                        for t in range(Q):
                            if scan_in(st):
                                turn_states(st, j, i, t)
                            for step in after.get((i, t), []):
                                step()

        @block.scalar
        def _(eng):
            started(eng, [ac_v, ac_th, ac_xd, ac_sp, ac_du, ac_z, ac_turn, ac_da, ac_h, ac_sc, ac_e, ac_out, s_out])
            def conv_first(st, j):
                q = j + Q * (st + 2)
                eng.wait_ge(pe_in, q + (START + 1))
                eng.wait_ge(ve_u, q + START)
                eng.activation(v[:, :], p_pr[:, :], ACT.Identity, bias=cb[:, bass.ds(j, 1)],
                               scale=cw[:, bass.ds(j, 1), TAPS - 1:TAPS].rearrange("p a b -> p (a b)")).then_inc(ac_v, 1)

            def tanh_v(st, j):
                q = j + Q * (st + 2)
                eng.wait_ge(ve_tap, q * 3 + (START + 3))
                eng.activation(th[:, :], v[:, :], ACT.Tanh).then_inc(ac_th, 1)

            def copy_small(b, uses):
                eng.wait_ge(pe_turn, START + uses + 1)
                eng.wait_ge(pe_dl, START + Q * b)
                eng.activation(xd[0:DR, :], p_rows[0:DR, :], ACT.Copy).then_inc(ac_xd, 1)
                if b:
                    eng.wait_ge(s_bst, 16 * b)
                eng.activation(bc[:, :], p_rows[BROW:BROW + 2 * NS, :], ACT.Copy).then_inc(ac_turn, 1)

            def copy_c(b, uses):
                eng.wait_ge(pe_turn, START + uses + 1)
                if b >= 2:
                    eng.wait_ge(ve_acc, START + Q * NS * (b - 1))
                eng.activation(c_t[:, b % 2, :, :], p_tr[:, :, NS:2 * NS], ACT.Copy).then_inc(ac_turn, 1)

            def softplus_tail(st, j, part):
                q = j + Q * (st + 1)
                if part == 0:
                    eng.wait_ge(pe_dl, q + (START + 1))
                    eng.wait_ge(ve_dl, q + START)
                    eng.activation(sp[:, :], p_pr[:, :], ACT.Abs).then_inc(ac_sp, 1)
                    eng.wait_ge(ac_sp, q * 3 + (START + 1))
                    eng.activation(sp[:, :], sp[:, :], ACT.Exp, scale=-1.0).then_inc(ac_sp, 1)
                else:
                    eng.wait_ge(ac_sp, q * 3 + (START + 2))
                    eng.activation(sp[:, :], sp[:, :], ACT.Ln, bias=1.0).then_inc(ac_sp, 1)

            def skip(st, j):
                q = j + Q * (st + 1)
                eng.wait_ge(ve_u, q + (START + 1))
                eng.activation(dut[:, :], u[:, bass.ds(j, 1), :].rearrange("p a l -> p (a l)"), ACT.Copy,
                               scale=dsk[:, bass.ds(j, 1)]).then_inc(ac_du, 1)

            def z_half(st, j, part):
                b, q = st, j + Q * st
                if part == 0:
                    eng.wait_ge(s_x[b % 3], 16 * (b // 3 + 1))
                    eng.wait_ge(po_z, q * 4 + (START + 4))
                    eng.wait_ge(ve_z, q + START)
                row = xs[:, b % 3, bass.ds(j, 1), :].rearrange("p a l -> p (a l)")
                eng.activation((zh, zt)[part][:, :], row, (ACT.Identity, ACT.Tanh)[part],
                               bias=zr[:, 3:4], scale=zr[:, 2:3]).then_inc(ac_z, 1)

            def copy_turn(dest, uses):
                eng.wait_ge(pe_turn, uses + (START + 1))
                eng.activation(dest, p_tr[:, :, :], ACT.Copy).then_inc(ac_turn, 1)

            def decay(st, j, i, k):
                b, m = st, i * Q + k
                eng.wait_ge(ve_scan, (j * NB + NS * st) * Q + (START + 1 + m - DA_AGO[m]))
                eng.activation(p_da[:, DA_BANK[m], :], delta[:, b % 2, k, :], ACT.Exp,
                               scale=a_neg[:, k, bass.ds(j * NB + i, 1)]).then_inc(ac_da, 1)

            def normed(st, j):
                f = j + Q * (st - 1)
                eng.wait_ge(po_f, f * 3 + (START + 3))
                eng.activation(h[:, :], x2[:, :], ACT.Identity, bias=fr[:, 2:3], scale=fr[:, 1:2]).then_inc(ac_h, 1)

            def copy_scores(st, j):
                f = j + Q * (st - 1)
                eng.wait_ge(pe_sc, f + (START + 1))
                eng.wait_ge(ve_g, f * 9 + START)
                eng.activation(sc[:, :], p_f[:, 0:S], ACT.Copy).then_inc(ac_sc, 1)

            def exp_scores(st, j):
                f = j + Q * (st - 1)
                eng.wait_ge(ve_top, f * 4 + (START + 2))
                eng.activation(ex[:, :], sc[:, :], ACT.Exp, bias=nmx[:, :], accum_out=z_sum[:, :]).then_inc(ac_e, 1)

            def copy_out(st, j):
                f = j + (Q * (st - 1) - 1)
                eng.wait_ge(pe_v, f + (START + 1))
                eng.wait_ge(s_out, f * 16 + START)
                eng.activation(ot[:, :], p_f[:, :], ACT.Copy).then_inc(ac_out, 1)
                eng.wait_ge(ac_out, f + (START + 1))
                eng.dma_start(out_rows[bass.ds(f * P, P), :], ot[:, :]).then_inc(s_out, 16)

            def conv_first_open(b, e):
                eng.wait_ge(pe_in, START + Q * b + e + 1)
                eng.activation(v_open[b][:, e, :], banks_open[b][e], ACT.Identity, bias=cb[:, e:e + 1],
                               scale=cw[:, e, TAPS - 1:TAPS]).then_inc(ac_v, 1)

            def tanh_open(b, e):
                eng.wait_ge(ve_tap, START + 3 * (Q * b + e + 1))
                eng.activation(th_open[b][:, e, :], v_open[b][:, e, :], ACT.Tanh).then_inc(ac_th, 1)

            eng.wait_ge(ve_c, 2)
            conv_first_open(0, 0)
            for e in range(1, Q):
                conv_first_open(0, e)
                tanh_open(0, e - 1)
            tanh_open(0, Q - 1)
            conv_first_open(1, 0)
            eng.wait_ge(po_c, 7)
            copy_small(0, 0)
            conv_first_open(1, 1)
            conv_first_open(1, 2)
            eng.wait_ge(s_second, 16 * 6)
            halves = [slice(0, Q // 2), slice(Q // 2, Q)]
            for i, half in enumerate(halves):
                eng.wait_ge(pe_dl, START + half.stop)
                eng.activation(sp_open[:, half, :], p_scan[:, half, :], ACT.Abs).then_inc(ac_sp, 2)
                eng.wait_ge(ac_sp, START + 4 * i + 2)
                eng.activation(sp_open[:, half, :], sp_open[:, half, :], ACT.Exp, scale=-1.0).then_inc(ac_sp, 2)
            eng.activation(a_neg[:, :, :], a_neg[:, :, :], ACT.Exp).then_inc(ac_c, 1)
            for i, half in enumerate(halves):
                eng.wait_ge(ac_sp, START + 4 * (i + 1))
                eng.activation(sp_open[:, half, :], sp_open[:, half, :], ACT.Ln, bias=1.0).then_inc(ac_sp, 2)
            conv_first_open(1, 3)
            tanh_open(1, 0)
            for e in range(Q):
                eng.wait_ge(ve_u, START + e + 1)
                eng.activation(dut_open[:, e, :], u[:, e, :], ACT.Copy, scale=dsk[:, e:e + 1]).then_inc(ac_du, 1)
            for e in range(Q):
                copy_turn(acc[:, 0, :, e * P:(e + 1) * P], 1 + e)
            copy_c(0, 1 + Q)
            for e in range(1, Q):
                tanh_open(1, e)
            eng.wait_ge(ve_c, 4)

            for run in RUNS:
                st = run[0]
                if scan_in(st) and run[1] == 0:
                    eng.wait_ge(ve_dl, START + Q * (st + 1))
                with each_turn(eng, run) as j:
                    after = {}

                    def put(at, step):
                        after.setdefault(at, []).append(step)

                    def copy_h():
                        eng.wait_ge(pe_hu, (j + Q * (st - 1)) + START)
                        copy_turn(h_t[:, :, :], turn(run, j, "h"))

                    def copy_du():
                        b = st + 1
                        if b == 1:
                            eng.wait_ge(ve_u, START + 2 * Q)
                        if b >= 3:
                            eng.wait_ge(ve_f, START + 4 * Q * (b - 2))
                        copy_turn(acc[:, b % 3, :, bass.ds(j * P, P)], turn(run, j, "du"))

                    def copy_z():
                        if st >= 2:
                            eng.wait_ge(ve_f, START + 4 * Q * (st - 1))
                        copy_turn(sz_t[:, st % 2, :, bass.ds(j * P, P)], turn(run, j, "z"))

                    def copy_gated():
                        f = j + Q * (st - 1)
                        eng.wait_ge(pe_v, f + START)
                        copy_turn(hug_t[:, :, :], turn(run, j, "hug"))

                    if prepare_in(st) and run[1] == 0:
                        put((0, 3), lambda: copy_small(st + 1, turn(run, j, "small")))
                    if ffn_end_in(st, run[1]):
                        put((1, 0), lambda: copy_out(st, j))
                    if ffn_in(st):
                        put((1, 1), lambda: normed(st, j))
                        put((2, 2), copy_h)
                        put((3, 0), lambda: copy_scores(st, j))
                    if project_in(st):
                        put((1, 3), lambda: conv_first(st, j))
                    if prepare_in(st):
                        put((0, 2), lambda: skip(st, j))
                        put((3, 1), copy_du)
                    if scan_in(st):
                        put((2, 0), lambda: z_half(st, j, 0))
                        put((2, 3), lambda: z_half(st, j, 1))
                    if prepare_in(st):
                        put((3, 2), lambda: softplus_tail(st, j, 0))
                    if prepare_in(st) and run[1] == 0:
                        put((3, 2), lambda: copy_c(st + 1, turn(run, j, "c")))
                    if ffn_in(st):
                        put((3, 3), lambda: exp_scores(st, j))
                    if project_in(st):
                        put((3, 3), lambda: tanh_v(st, j))
                    if prepare_in(st):
                        put((3, 3), lambda: softplus_tail(st, j, 1))
                    if scan_in(st):
                        put((3, 3), copy_z)
                    if ffn_in(st):
                        put((3, 3), copy_gated)
                    for i in range(NB):
                        for k in range(Q):
                            if scan_in(st):
                                decay(st, j, i, k)
                            for step in after.get((i, k), []):
                                step()
                if run == (0, 0, 1):
                    eng.wait_ge(s_w, 16 * 5)
                    eng.activation(gx[:, :], gx[:, :], ACT.Tanh).then_inc(ac_c, 1)
                    eng.activation(gf[:, :], gf[:, :], ACT.Tanh).then_inc(ac_c, 1)
                    eng.wait_ge(pe_c, 1)
                    eng.activation(aw[:, :], p_f[:, 0:S], ACT.Exp, scale=-1.0).then_inc(ac_c, 1)
            eng.wait_ge(s_out, START + 16 * Q * B)

        @block.vector
        def _(eng):
            started(eng, [ve_tap, ve_u, ve_dl, ve_zs, ve_z, ve_scan, ve_acc, ve_f, ve_top, ve_g, ve_hug])
            eng.wait_ge(s_conv, 32)
            eng.tensor_scalar(cw[:, :, :], cw[:, :, :], 0.5, None, ALU.mult).then_inc(ve_c, 1)
            eng.tensor_scalar(cb[:, :], cb[:, :], 0.5, None, ALU.mult).then_inc(ve_c, 1)
            eng.wait_ge(ve_c, 2)

            def taps(q, j, v, bank, which=range(1, TAPS)):
                if 1 in which:
                    eng.wait_ge(ac_v, q + (START + 1))
                for s in which:
                    if s > 1:
                        eng.wait_ge(ve_tap, q * 3 + (START + s - 1))
                    eng.scalar_tensor_tensor(
                        out=v[:, s:], in0=bank[:, 0:L - s], in1=v[:, s:], op0=ALU.mult, op1=ALU.add,
                        scalar=cw[:, bass.ds(j, 1), TAPS - 1 - s:TAPS - s].rearrange("p a b -> p (a b)"),
                    ).then_inc(ve_tap, 1)

            def silu_u(b, j, v, th):
                q = j + Q * b
                eng.wait_ge(ac_th, q + (START + 1))
                if b:
                    eng.wait_ge(pe_turn, START + (turns_before((b - 2, 0, 1)) if b > 1 else 0) + 1)
                    eng.wait_ge(po_du, q + (START - Q + 1))
                    eng.wait_ge(ac_du, q + (START - Q + 1))
                eng.scalar_tensor_tensor(out=u[:, bass.ds(j, 1), :].rearrange("p a l -> p (a l)"), in0=th,
                                         scalar=1.0, in1=v, op0=ALU.add, op1=ALU.mult).then_inc(ve_u, 1)

            def softplus(st, j):
                b, q = st + 1, j + Q * (st + 1)
                eng.wait_ge(ac_sp, q * 3 + (START + 3))
                if b >= 2:
                    eng.wait_ge(ac_da, START + Q * NS * (b - 1))
                    eng.wait_ge(po_du, START + Q * (b - 1))
                eng.scalar_tensor_tensor(out=delta[:, b % 2, bass.ds(j, 1), :].rearrange("p a l -> p (a l)"),
                                         in0=p_pr[:, :], scalar=0.0, in1=sp[:, :], op0=ALU.max,
                                         op1=ALU.add).then_inc(ve_dl, 1)

            def z_statistics(st, j, part):
                b, q = st, j + Q * st
                if part == 0:
                    eng.wait_ge(s_x[b % 3], 16 * (b // 3 + 1))
                    eng.wait_ge(ve_zs, q * 2 + START)
                    eng.bn_stats(zst[:, :], xs[:, b % 3, bass.ds(j, 1), :].rearrange("p a l -> p (a l)")).then_inc(ve_zs, 1)
                else:
                    eng.wait_ge(ve_zs, q * 2 + (START + 1))
                    eng.wait_ge(po_z, q * 4 + START)
                    eng.sem_inc(stood, 1)
                    eng.bn_aggr(zmv[:, :], zst[:, :]).then_inc(ve_zs, 1)

            def silu_z(st, j):
                q = j + Q * st
                eng.wait_ge(ac_z, q * 2 + (START + 2))
                eng.scalar_tensor_tensor(out=zh[:, :], in0=zt[:, :], scalar=1.0, in1=zh[:, :], op0=ALU.add,
                                         op1=ALU.mult).then_inc(ve_z, 1)

            def scan(st, j, i, k):
                n = j * NB + NS * st + i
                if k == 0:
                    eng.wait_ge(po_dbu, n + (START + 1))
                    eng.wait_ge(pe_st, (n - 1) * Q + START)
                eng.wait_ge(ac_da, n * Q + (START + k + 1))
                eng.tensor_tensor_scan(state[:, i % 2, k, :], p_da[:, DA_BANK[i * Q + k], :], dbu[:, i % 2, k, :], 0.0,
                                       ALU.mult, ALU.add).then_inc(ve_scan, 1)

            def accumulate(st, j, i, t):
                b, n = st, j * NB + NS * st + i
                eng.wait_ge(pe_st, n * Q + (START + t + 1))
                eng.wait_ge(ve_acc, n * Q + (START + t - Q + 1))
                eng.scalar_tensor_tensor(out=acc[:, b % 3, t, :], in0=p_st[:, t % 2, :],
                                         scalar=c_t[:, b % 2, t, bass.ds(j * NB + i, 1)], in1=acc[:, b % 3, t, :],
                                         op0=ALU.mult, op1=ALU.add).then_inc(ve_acc, 1)

            def residual(st, j, meanwhile):
                b, f = st - 1, j + Q * (st - 1)
                block_b = lambda t, depth: t[:, b % depth, bass.ds(j, 1), :].rearrange("p a l -> p (a l)")
                eng.wait_ge(ve_f, f * 4 + START)
                eng.tensor_tensor(fm[:, :], block_b(acc, 3), block_b(sz_t, 2), ALU.mult).then_inc(ve_f, 1)
                for step in meanwhile[:-1]:
                    step()
                eng.wait_ge(ve_f, f * 4 + (START + 1))
                eng.wait_ge(ac_h, f + START)
                eng.wait_ge(pe_x2, f + START)
                eng.scalar_tensor_tensor(out=x2[:, :], in0=fm[:, :], scalar=gx[:, :],
                                         in1=xs[:, b % 3, bass.ds(j, 1), :].rearrange("p a l -> p (a l)"),
                                         op0=ALU.mult, op1=ALU.add).then_inc(ve_f, 1)
                for step in meanwhile[-1:]:
                    step()
                eng.wait_ge(ve_f, f * 4 + (START + 2))
                eng.bn_stats(fst[:, :], x2[:, :]).then_inc(ve_f, 1)

            def residual_statistics(st, j):
                f = j + Q * (st - 1)
                eng.wait_ge(ve_f, f * 4 + (START + 3))
                eng.wait_ge(po_f, f * 3 + START)
                eng.sem_inc(stood, 1)
                eng.bn_aggr(fmv[:, :], fst[:, :]).then_inc(ve_f, 1)

            def best_two(st, j):
                f = j + Q * (st - 1)
                eng.wait_ge(ac_sc, f + (START + 1))
                eng.wait_ge(ve_g, f * 9 + START)
                eng.sem_inc(stood, 1)
                eng.max(top[:, :], sc[:, :]).then_inc(ve_top, 1)
                eng.wait_ge(ve_top, f * 4 + (START + 1))
                eng.wait_ge(ac_e, f + START)
                eng.tensor_scalar(nmx[:, :], top[:, 0:1], -1.0, None, ALU.mult).then_inc(ve_top, 1)
                eng.max_index(top_i[:, :], top[:, :], sc[:, :]).then_inc(ve_top, 1)
                eng.wait_ge(ve_top, f * 4 + (START + 3))
                eng.tensor_copy(top_f[:, :], top_i[:, 0:2]).then_inc(ve_top, 1)

            def gates(st, j, meanwhile):
                f = j + Q * (st - 1)
                made = lambda n: eng.wait_ge(ve_g, f * 9 + (START + n))
                eng.wait_ge(ac_e, f + (START + 1))
                eng.wait_ge(ve_top, f * 4 + (START + 4))
                eng.wait_ge(ve_hug, f + START)
                eng.scalar_tensor_tensor(out=e1[:, :], in0=iota_f[:, :], scalar=top_f[:, 0:1], in1=ex[:, :],
                                         op0=ALU.is_equal, op1=ALU.mult).then_inc(ve_g, 1)
                eng.scalar_tensor_tensor(out=e2[:, :], in0=iota_f[:, :], scalar=top_f[:, 1:2], in1=ex[:, :],
                                         op0=ALU.is_equal, op1=ALU.mult).then_inc(ve_g, 1)
                made(2)
                eng.scalar_tensor_tensor(out=em[:, :], in0=e1[:, :], scalar=1.0, in1=e2[:, :], op0=ALU.mult,
                                         op1=ALU.add, accum_out=ga[:, 0:1]).then_inc(ve_g, 1)
                made(3)
                eng.scalar_tensor_tensor(out=ga[:, 1:2], in0=z_sum[:, :], scalar=GATE_EPS, in1=ga[:, 0:1],
                                         op0=ALU.mult, op1=ALU.add).then_inc(ve_g, 1)
                eng.scalar_tensor_tensor(out=gsc[:, :], in0=em[:, :], scalar=1.0, in1=aw[:, :], op0=ALU.mult,
                                         op1=ALU.mult, accum_out=ga[:, 3:4]).then_inc(ve_g, 1)
                for step in meanwhile[0:1]:
                    step()
                made(5)
                eng.reciprocal(ga[:, 2:3], ga[:, 1:2]).then_inc(ve_g, 1)
                for step in meanwhile[1:2]:
                    step()
                made(6)
                eng.tensor_scalar(ga[:, 4:5], ga[:, 3:4], ga[:, 2:3], 0.2, ALU.mult, ALU.mult).then_inc(ve_g, 1)
                made(7)
                eng.tensor_scalar(ga[:, 5:6], ga[:, 4:5], 0.9, ga[:, 2:3], ALU.add, ALU.mult).then_inc(ve_g, 1)
                made(8)
                eng.tensor_scalar(gw[:, :], em[:, :], ga[:, 5:6], gf[:, :], ALU.mult, ALU.mult).then_inc(ve_g, 1)
                made(9)
                eng.wait_ge(pe_hu, f + (START + 1))
                eng.tensor_tensor(hug[:, :, :], p_f[:, :].rearrange("p (s r) -> p s r", r=R),
                                  gw[:, :].unsqueeze(2).to_broadcast([P, S, R]), ALU.mult).then_inc(ve_hug, 1)

            def taps_open(b, e):
                taps(Q * b + e, e, v_open[b][:, e, :], banks_open[b][e])

            def silu_u_open(b, e):
                silu_u(b, e, v_open[b][:, e, :], th_open[b][:, e, :])

            taps_open(0, 0)
            for e in range(1, Q):
                taps_open(0, e)
                silu_u_open(0, e - 1)
            silu_u_open(0, Q - 1)
            taps_open(1, 0)
            taps_open(1, 1)
            eng.wait_ge(s_w, 16 * 5)
            eng.wait_ge(po_c, 7)
            eng.tensor_copy(wa_wide[:, :], wa_sb[:, :].to_broadcast([AD, P])).then_inc(ve_c, 1)
            eng.wait_ge(ac_c, 1)
            eng.tensor_scalar(a_neg[:, :, :], a_neg[:, :, :], -1.0, None, ALU.mult).then_inc(ve_c, 1)
            eng.tensor_copy(iota_f[:, :], iota_i[:, :]).then_inc(ve_c, 1)
            for i, half in enumerate([slice(0, Q // 2), slice(Q // 2, Q)]):
                eng.wait_ge(ac_sp, START + 10 + 2 * i)
                eng.scalar_tensor_tensor(out=delta[:, 0, half, :], in0=p_scan[:, half, :], scalar=0.0,
                                         in1=sp_open[:, half, :], op0=ALU.max, op1=ALU.add).then_inc(ve_dl, 2)
            taps_open(1, 2)
            taps_open(1, 3)
            silu_u_open(1, 0)
            for e in range(1, Q):
                silu_u_open(1, e)

            for run in RUNS:
                st = run[0]
                if (scan_in(st) or ffn_in(st)) and run[1] == 0:
                    eng.wait_ge(ac_turn, START + turns_before((st, 0, 1)) - ffn_in(st - 1))
                if st == 1 and run[1] == 0:
                    eng.wait_ge(ac_c, 4)
                    eng.tensor_scalar(aw[:, :], aw[:, :], 1.0, None, ALU.add).then_inc(ve_c, 1)
                    eng.wait_ge(ve_c, 6)
                    eng.reciprocal(aw[:, :], aw[:, :]).then_inc(ve_c, 1)
                    eng.wait_ge(ve_c, 7)
                with each_turn(eng, run) as j:
                    between = {}

                    def put(at, step):
                        between.setdefault(at, []).append(step)

                    if ffn_in(st) and scan_in(st):
                        put((0, 0), lambda: residual_statistics(st, j))
                    if project_in(st):
                        for s in range(1, TAPS):
                            put([(1, 2), (1, 3), (2, 0)][s - 1], lambda s=s: taps(j + Q * (st + 2), j, v[:, :], p_pr[:, :], [s]))
                        if run[1] > 0:
                            put((0, 3), lambda: silu_u(st + 2, j - 1, v[:, :], th[:, :]))
                    if ffn_in(st):
                        put((3, 1), lambda: best_two(st, j))
                    if scan_in(st):
                        put((3, 0), lambda: silu_z(st, j))

                    statistics = [lambda part=part: z_statistics(st, j, part) for part in (0, 1)] if scan_in(st) else []
                    late = [lambda t=t: accumulate(st, j, -1, t) for t in range(2, Q)] if scan_in(st) and run[1] > 0 else []
                    if ffn_in(st):
                        residual(st, j, statistics[:1] + late + statistics[1:])
                        late = []
                        if not scan_in(st):
                            residual_statistics(st, j)
                    else:
                        for step in statistics:
                            step()
                    for i in range(NB):
                        for k in range(Q):
                            if scan_in(st):
                                scan(st, j, i, k)
                                if i:
                                    accumulate(st, j, i - 1, k)
                                elif k < len(late):
                                    late[k]()
                            for step in between.get((i, k), []):
                                step()
                    last = [lambda t=t: accumulate(st, j, NB - 1, t) for t in range(2)] if scan_in(st) else []
                    if ffn_in(st):
                        gates(st, j, last)
                        last = []
                    for step in last:
                        step()
                    if prepare_in(st):
                        softplus(st, j)
                if scan_in(st) and run[2] == Q:
                    for t in range(2, Q):
                        accumulate(st, Q - 1, NB - 1, t)
                if project_in(st) and run[2] == Q:
                    silu_u(st + 2, Q - 1, v[:, :], th[:, :])


def kernel(**inputs):
    import numpy as _np
    import concourse.bacc as _bacc
    from concourse import mybir as _mybir
    from concourse.bass_utils import run_bass_kernel_spmd as _run

    given = {k: _np.asarray(a) for k, a in inputs.items()}
    s, hdim, r = given["L0_ffn_U"].shape
    arrays = {
        "x": given["x"],
        "ctx_t": given["ctx_1024"].transpose(0, 2, 1),
        "g_xattn": given["g_xattn"],
        "g_ffn": given["g_ffn"],
        "in_w_t": given["L0_xattn_in_proj_w"].T,
        "conv_w": given["L0_xattn_conv_w"],
        "conv_b": given["L0_xattn_conv_b"],
        "x_w_t": given["L0_xattn_x_proj_w"].T,
        "dt_w_t": given["L0_xattn_dt_proj_w"].T,
        "dt_b": given["L0_xattn_dt_proj_b"],
        "a_log": given["L0_xattn_A_log"],
        "d_skip": given["L0_xattn_D"],
        "router_t": given["L0_ffn_Wr"].T,
        "u_w": given["L0_ffn_U"].transpose(1, 0, 2).reshape(hdim, s * r),
        "v_w": given["L0_ffn_V"].reshape(s * r, hdim),
        "attr_t": given["L0_ffn_attr"].T,
        "attr_w": given["L0_ffn_Wa"],
    }
    nc = _bacc.Bacc("TRN2", target_bir_lowering=False, num_devices=1)
    maps, args = {}, []
    for name, a in arrays.items():
        a = _np.ascontiguousarray(a)
        maps[f"in_{name}"] = a
        args.append(nc.dram_tensor(f"in_{name}", a.shape, _mybir.dt.from_np(a.dtype), kind="ExternalInput").ap())
    args.append(nc.dram_tensor("out_0", given["x"].shape, _mybir.dt.float32, kind="ExternalOutput").ap())
    flamingo(nc, *args)
    got = _run(nc, [maps], core_ids=[0])
    return got.results[0]["out_0"]
```

```python
from contextlib import ExitStack, nullcontext

import concourse.bass as bass
from concourse import mybir

ALU = mybir.AluOpType
ACT = mybir.ActivationFunctionType
F32 = mybir.dt.float32
I32 = mybir.dt.int32
U32 = mybir.dt.uint32

P = 128
Q = 4
EPS = 1e-5
GATE_EPS = 1e-8
START = 16


def flamingo(nc, x, ctx_t, g_xattn, g_ffn, in_w_t, conv_w, conv_b, x_w_t, dt_w_t, dt_b, a_log, d_skip,
             router_t, u_w, v_w, attr_t, attr_w, out):
    B, L, E = x.shape
    DM = ctx_t.shape[1]
    KD = DM // P
    DR = dt_w_t.shape[0]
    NS = a_log.shape[1]
    S = router_t.shape[1]
    R = u_w.shape[1] // S
    AD = attr_t.shape[0]
    TAPS = conv_w.shape[1]
    BROW = 32
    NB = NS // Q
    assert L == E == Q * P and NB == 4 and S * R == Q * P and TAPS == 4

    RUNS = [run for st in range(B) for run in ((st, 0, 1), (st, 1, Q))]
    CLOSING = (B, 0, 1)

    def project_in(st):
        return 0 <= st + 2 < B

    def prepare_in(st):
        return 0 <= st + 1 < B

    def scan_in(st):
        return 0 <= st < B

    def ffn_in(st):
        return 0 <= st - 1 < B

    def ffn_end_in(st, j0):
        return 0 <= Q * (st - 1) + j0 - 1 < Q * B

    def turn_kinds(run):
        st = run[0]
        first = prepare_in(st) and run[1] == 0
        return (["small"] * first + ["h"] * ffn_in(st) + ["du"] * prepare_in(st) + ["c"] * first
                + ["z"] * scan_in(st) + ["hug"] * ffn_in(st))

    OPENING_KINDS = ["small"] + ["du"] * Q + ["c"]

    def turns_before(run):
        return len(OPENING_KINDS) + sum((r[2] - r[1]) * len(turn_kinds(r)) for r in RUNS if r < run)

    def turn(run, j, kind):
        first = turns_before(run) + (turn_kinds(run).index(kind) if kind else 0)
        return (j - run[1]) * len(turn_kinds(run)) + first

    def each_turn(eng, run):
        return eng.Fori(run[1], run[2]) if run[2] - run[1] > 1 else nullcontext(run[1])

    with ExitStack() as ctx:
        def sb(name, shape, dt=F32):
            return ctx.enter_context(nc.sbuf_tensor(name, shape, dt))

        def psum(name, shape):
            return ctx.enter_context(nc.psum_tensor(name, shape, F32))

        def sem(name):
            return ctx.enter_context(nc.semaphore(name))

        ident = sb("ident", [P, P])
        iota_i = sb("iota_i", [P, S], I32)
        iota_f = sb("iota_f", [P, S])
        eps_c = sb("eps_c", [P, 1])
        minus_half = sb("minus_half", [P, 1])
        table = sb("table", [P, 1])
        a_neg = sb("a_neg", [P, Q, NS])
        cw = sb("cw", [P, Q, TAPS])
        cb = sb("cb", [P, Q])
        dsk = sb("dsk", [P, Q])
        w_small = sb("w_small", [P, Q, BROW + 2 * NS])
        w_in = sb("w_in", [P, KD, P])
        w_dt = sb("w_dt", [DR + 1, P])
        router = sb("router", [P, Q, S])
        u_sb = sb("u_sb", [P, Q, S * R])
        v_sb = sb("v_sb", [P, Q, E])
        at_sb = sb("at_sb", [AD, S])
        wa_sb = sb("wa_sb", [AD, 1])
        wa_wide = sb("wa_wide", [AD, P])
        aw = sb("aw", [P, S])
        gx = sb("gx", [P, 1])
        gf = sb("gf", [P, 1])
        xs = sb("xs", [P, 3, Q, L])
        cx = sb("cx", [P, 2, KD, L])
        v = sb("v", [P, L])
        th = sb("th", [P, L])
        u = sb("u", [P, Q, L])
        xd = sb("xd", [DR + 1, L])
        bc = sb("bc", [2 * NS, L])
        c_t = sb("c_t", [P, 2, Q, NS])
        sp = sb("sp", [P, L])
        delta = sb("delta", [P, 2, Q, L])
        du = sb("du", [P, 2, Q, L])
        dut = sb("dut", [P, L])
        zst = sb("zst", [P, 6])
        zmv = sb("zmv", [P, 2])
        zr = sb("zr", [P, 4])
        zh = sb("zh", [P, L])
        zt = sb("zt", [P, L])
        sz_t = sb("sz_t", [P, 2, Q, E])
        bbc = sb("bbc", [P, 4, L])
        dbu = sb("dbu", [P, 2, Q, L])
        state = sb("state", [P, 2, Q, L])
        acc = sb("acc", [P, 3, Q, E])
        fm = sb("fm", [P, E])
        x2 = sb("x2", [P, E])
        fst = sb("fst", [P, 6])
        fmv = sb("fmv", [P, 2])
        fr = sb("fr", [P, 3])
        h = sb("h", [P, E])
        h_t = sb("h_t", [P, Q, P])
        sc = sb("sc", [P, S])
        top = sb("top", [P, 8])
        top_i = sb("top_i", [P, 8], U32)
        top_i_close = sb("top_i_close", [P, Q, 8], U32)
        top_f = sb("top_f", [P, 2])
        nmx = sb("nmx", [P, 1])
        ex = sb("ex", [P, S])
        z_sum = sb("z_sum", [P, 1])
        e1 = sb("e1", [P, S])
        e2 = sb("e2", [P, S])
        em = sb("em", [P, S])
        ga = sb("ga", [P, 8])
        gsc = sb("gsc", [P, S])
        gw = sb("gw", [P, S])
        hug = sb("hug", [P, S, R])
        hug_t = sb("hug_t", [P, Q, P])
        ot = sb("ot", [P, E])
        out_rows = out.rearrange("b l e -> (b l) e")
        b_rows = nc.dram_tensor("b_rows", [B * NS, L], F32).ap()

        p_scan = psum("p_scan", [P, 5, L])
        p_da = p_scan[:, 0:3, :]
        p_st = p_scan[:, 3:5, :]
        p_pr = psum("p_pr", [P, L])
        p_tr = psum("p_tr", [P, Q, P])
        p_rows = p_tr[:, :, :].rearrange("p t m -> p (t m)")
        p_f = psum("p_f", [P, E])

        s_w = sem("weights_loaded")
        s_x = [sem(f"x_loaded{i}") for i in range(3)]
        s_cx = [sem(f"ctx_loaded{i}") for i in range(2)]
        s_uv = sem("u_v_loaded")
        s_first = sem("in_projection_weights_loaded")
        s_rest = sem("in_projection_weights_loaded_rest")
        s_conv = sem("conv_weights_loaded")
        s_second = sem("prepare_weights_loaded")
        s_win = sem("w_in_loaded")
        s_wdt = sem("w_dt_loaded")
        s_bst = sem("b_stored")
        s_bbc = [sem(f"b_broadcast{i}") for i in range(4)]
        s_out = sem("out_stored")
        s_last = sem("last_batch_stored")
        po_c = sem("pool_constants")
        ve_c = sem("dve_constants")
        stood = sem("stood")
        ac_c = sem("act_constants")
        pe_c = sem("pe_constants")
        pe_in = sem("pe_in_projected")
        pe_dl = sem("pe_dt_projected")
        pe_turn = sem("pe_turned")
        pe_st = sem("pe_states_turned")
        pe_sc = sem("pe_scores")
        pe_hu = sem("pe_hu")
        pe_x2 = sem("pe_x2")
        pe_v = sem("pe_v")
        ac_v = sem("act_conv_started")
        ac_th = sem("act_tanh_v")
        ac_xd = sem("act_small_copied")
        ac_sp = sem("act_softplus")
        ac_du = sem("act_d_u")
        ac_z = sem("act_z")
        ac_turn = sem("act_turn_copied")
        ac_da = sem("act_decay")
        ac_h = sem("act_h")
        ac_sc = sem("act_scores_copied")
        ac_e = sem("act_exp_scores")
        ac_out = sem("act_out")
        ve_tap = sem("dve_taps")
        ve_u = sem("dve_u")
        ve_dl = sem("dve_delta")
        ve_zs = sem("dve_z_statistics")
        ve_scan = sem("dve_scanned")
        ve_acc = sem("dve_accumulated")
        ve_f = sem("dve_residual_statistics")
        ve_top = sem("dve_top")
        ve_g = sem("dve_gates")
        ve_hug = sem("dve_gated")
        po_dbu = sem("pool_dbu")
        po_du = sem("pool_du")
        po_f = sem("pool_f_scale")
        po_sz = sem("pool_silu_z")
        yz_made = sem("y_times_z")
        po_z = sem("pool_z_scale")

        w_in_all = xs[:, 2, 0:KD, :]
        w_dt_all = xs[0:DR + 1, 2, KD, :]
        v_open = [sz_t[:, 1], sz_t[:, 0]]
        th_open = [acc[:, 2], acc[:, 1]]
        dut_open = state[:, 0]
        sp_open = state[:, 1]
        banks_open = [[p_scan[:, e, :] for e in range(Q)],
                      [p_scan[:, 4, :], p_pr[:, :], p_f[:, :], p_scan[:, 4, :]]]

        x2_close, h_close = dbu[:, 0], dbu[:, 1]
        ht_close, hug_close = delta[:, 0], delta[:, 1]
        hugt_close, fm_close = du[:, 0], du[:, 1]
        ot_close = state[:, 0]
        close_turn = [p_rows, p_pr[:, :]]
        close_scores = [p_scan[:, 4, :], p_f[:, :]]

        def small_close(t, place, width):
            return bbc[:, t, place:place + width]

        def stats_close(t): return small_close(t, 0, 6)
        def mv_close(t): return small_close(t, 8, 2)
        def fr_close(t): return small_close(t, 12, 3)
        def top_close(t): return small_close(t, 16, 8)
        def topf_close(t): return small_close(t, 24, 2)
        def nmx_close(t): return small_close(t, 28, 1)
        def sum_close(t): return small_close(t, 30, 1)
        def ga_close(t): return small_close(t, 32, 8)
        def wide_close(t, which): return small_close(t, 64 + which * S, S)
        SC, EX, E1, E2, EM, GSC, GW = range(7)

        DA_BANK = [m % 3 for m in range(Q * NB - 1)] + [1]
        DA_AGO = [4, 2, 4] + [3] * (Q * NB - 4) + [2]
        for m in range(Q * NB):
            assert (DA_BANK + DA_BANK)[m:m + Q * NB + 1][::-1].index(DA_BANK[m], 1) == DA_AGO[m]

        cl_res = [sem(f"closing_dve_residual{t}") for t in range(Q)]
        cl_top = [sem(f"closing_dve_top{t}") for t in range(Q)]
        cl_gate = [sem(f"closing_dve_gates{t}") for t in range(Q)]
        cl_scale = [sem(f"closing_pool_scale{t}") for t in range(Q)]
        cl_h = sem("closing_act_h")
        cl_pe_h = sem("closing_pe_h_turned")
        cl_h_copied = sem("closing_act_h_copied")
        cl_sc = sem("closing_pe_scores")
        cl_sc_copied = sem("closing_act_scores_copied")
        cl_hu = sem("closing_pe_hu")
        cl_ex = sem("closing_act_exp")
        cl_hug = sem("closing_dve_gated")
        cl_pe_hug = sem("closing_pe_gated_turned")
        cl_hug_copied = sem("closing_act_gated_copied")
        cl_v = sem("closing_pe_v")
        cl_out = sem("closing_dve_out")

        N_W = 5

        block = ctx.enter_context(nc.Block())

        def started(eng, sems):
            for s in sems:
                eng.sem_inc(s, START)

        @block.sync
        def _(eng):
            def load_x(b):
                eng.dma_start(xs[:, b % 3], x[b].rearrange("(c p) l -> p c l", p=P)).then_inc(s_x[b % 3], 16)

            def load_ctx(b):
                eng.dma_start(cx[:, b % 2], ctx_t[b].rearrange("(k p) l -> p k l", p=P)).then_inc(s_cx[b % 2], 16)

            w_in_blocks = in_w_t.rearrange("(k p) e -> p k e", p=P)
            eng.dma_start(w_in_all[:, :, 0:P], w_in_blocks[:, :, 0:P]).then_inc(s_first, 16)
            load_ctx(0)
            eng.dma_start(w_in_all[:, :, P:], w_in_blocks[:, :, P:]).then_inc(s_rest, 16)
            eng.dma_start(cw[:, :, :], conv_w.rearrange("(c p) k -> p c k", p=P)).then_inc(s_conv, 16)
            with nc.allow_non_contiguous_dma(reason="one number for each channel"):
                eng.dma_start(cb[:, :], conv_b.rearrange("(c p) -> p c", p=P)).then_inc(s_conv, 16)
                eng.dma_start(dsk[:, :], d_skip.rearrange("(c p) -> p c", p=P)).then_inc(s_second, 16)
            by_channel = x_w_t.rearrange("(c p) k -> p c k", p=P)
            eng.dma_start(w_small[:, :, 0:DR], by_channel[:, :, 0:DR]).then_inc(s_second, 16)
            eng.dma_start(w_small[:, :, BROW:], by_channel[:, :, DR:]).then_inc(s_second, 16)
            eng.dma_start(w_dt_all[0:DR, :], dt_w_t).then_inc(s_second, 16)
            eng.dma_start(w_dt_all[DR:DR + 1, :], dt_b.rearrange("(a e) -> a e", a=1)).then_inc(s_second, 16)
            eng.dma_start(a_neg[:, :, :], a_log.rearrange("(c p) n -> p c n", p=P)).then_inc(s_second, 16)
            load_ctx(1)
            load_x(0)
            eng.dma_start(router[:, :, :], router_t.rearrange("(c p) s -> p c s", p=P)).then_inc(s_w, 16)
            eng.dma_start(at_sb[:, :], attr_t).then_inc(s_w, 16)
            with nc.allow_non_contiguous_dma(reason="one number for each partition"):
                eng.dma_start(wa_sb[:, :], attr_w.rearrange("a k -> k a")).then_inc(s_w, 16)
                eng.dma_start(gx[:, :], g_xattn.partition_broadcast(P)).then_inc(s_w, 16)
                eng.dma_start(gf[:, :], g_ffn.partition_broadcast(P)).then_inc(s_w, 16)

            def store_b(b):
                first = turns_before((b - 1, 0, 1)) if b else 0
                eng.wait_ge(ac_turn, START + first + 1)
                eng.dma_start(b_rows[b * NS:(b + 1) * NS, :], bc[0:NS, :]).then_inc(s_bst, 16)

            eng.wait_ge(pe_in, START + Q)
            load_ctx(2)
            load_x(1)
            eng.dma_start(u_sb[:, :, :], u_w.rearrange("(c p) n -> p c n", p=P)).then_inc(s_uv, 16)
            store_b(0)
            in_blocks = in_w_t.rearrange("(k p) e -> p k e", p=P)
            dt_bias = dt_b.rearrange("(a e) -> a e", a=1)
            for run in RUNS:
                st = run[0]
                if scan_in(st):
                    eng.wait_ge(s_bst, 16 * (st + 1))
                if not (prepare_in(st) or project_in(st) or scan_in(st)):
                    continue
                with each_turn(eng, run) as j:
                    if scan_in(st):
                        for i in range(NB):
                            n = j * NB + NS * st + i
                            eng.wait_ge(po_dbu, n - 3 + START)
                            row = b_rows[bass.ds(n, 1), :].rearrange("a l -> (a l)")
                            eng.dma_start(bbc[:, i, :], row.partition_broadcast(P)).then_inc(s_bbc[i], 16)
                    if project_in(st):
                        q = j + Q * (st + 2)
                        eng.wait_ge(pe_in, q + START)
                        eng.dma_start(w_in[:, :, :], in_blocks[:, :, bass.ds(j * P, P)]).then_inc(s_win, 16)
                    if prepare_in(st):
                        q = j + Q * (st + 1)
                        eng.wait_ge(pe_dl, q + START)
                        eng.dma_start(w_dt[0:DR, :], dt_w_t[:, bass.ds(j * P, P)]).then_inc(s_wdt, 16)
                        eng.dma_start(w_dt[DR:DR + 1, :], dt_bias[:, bass.ds(j * P, P)]).then_inc(s_wdt, 16)
                if run[2] == Q and prepare_in(st):
                    store_b(st + 1)
                if run[1] > 0:
                    continue
                if st == 0:
                    eng.dma_start(v_sb[:, :, :], v_w.rearrange("(c p) n -> p c n", p=P)).then_inc(s_uv, 16)
                    eng.wait_ge(pe_in, START + 2 * Q)
                    eng.wait_ge(pe_dl, START + Q)
                    load_x(2)
                if project_in(st + 1):
                    eng.wait_ge(pe_in, START + Q * (st + 2))
                    load_ctx(st + 3)
                if 3 <= st + 1 < B:
                    eng.wait_ge(ve_f, START + 3 * Q * (st - 1))
                    load_x(st + 1)
            for t in range(Q):
                eng.wait_ge(cl_out, t + 1)
                eng.dma_start(out_rows[((B - 1) * Q + t) * P:((B - 1) * Q + t + 1) * P, :],
                              ot_close[:, t, :]).then_inc(s_last, 16)
            eng.wait_ge(s_last, 16 * Q)

        @block.gpsimd
        def _(eng):
            started(eng, [po_dbu, po_du, po_f, yz_made, po_sz, po_z])
            eng.memset(w_small[:, :, DR:BROW], 0.0).then_inc(po_c, 1)
            eng.memset(ident[:, :], 0.0).then_inc(po_c, 1)
            eng.memset(xd[:, :], 1.0).then_inc(po_c, 1)
            eng.memset(eps_c[:, :], EPS).then_inc(po_c, 1)
            eng.memset(minus_half[:, :], -0.5).then_inc(po_c, 1)
            eng.iota(iota_i[:, :], [[1, S]], base=0, channel_multiplier=0).then_inc(po_c, 1)
            eng.wait_ge(po_c, 6)
            eng.affine_select(out=ident[:, :], in_=ident[:, :], compare_op=ALU.not_equal, fill=1.0, base=0,
                              pattern=[[-1, P]], channel_multiplier=1).then_inc(po_c, 1)

            def times_b(st, j, i, blocks=slice(0, Q)):
                b, n = st, j * NB + NS * st + i
                eng.wait_ge(s_bbc[i], (j + (Q * b + 1)) * 16)
                eng.wait_ge(ve_scan, (n - 1) * Q + START)
                made = eng.tensor_tensor(dbu[:, i % 2, blocks, :], du[:, b % 2, blocks, :],
                                         bbc[:, i:i + 1, :].to_broadcast([P, blocks.stop - blocks.start, L]), ALU.mult)
                if blocks.stop == Q:
                    made.then_inc(po_dbu, 1)

            def scale_of_f(st, j):
                f = j + Q * (st - 1)
                eng.wait_ge(ve_f, f * 3 + (START + 3))
                eng.wait_ge(ac_h, f + START)
                eng.tensor_tensor(fr[:, 0:1], fmv[:, 1:2], eps_c[:, :], ALU.add).then_inc(po_f, 1)
                eng.wait_ge(po_f, f * 3 + (START + 1))
                eng.tensor_tensor(fr[:, 1:2], fr[:, 0:1], minus_half[:, :], ALU.pow).then_inc(po_f, 1)
                eng.wait_ge(po_f, f * 3 + (START + 2))
                eng.sem_inc(stood, 1)
                eng.tensor_scalar(fr[:, 2:3], fmv[:, 0:1], fr[:, 1:2], -1.0, ALU.mult, ALU.mult).then_inc(po_f, 1)

            def scale_of_z(st, j):
                q = j + Q * st
                eng.wait_ge(ve_zs, q * 2 + (START + 2))
                eng.wait_ge(ac_z, q * 2 + START)
                eng.tensor_tensor(zr[:, 0:1], zmv[:, 1:2], eps_c[:, :], ALU.add).then_inc(po_z, 1)
                eng.wait_ge(po_z, q * 4 + (START + 1))
                eng.tensor_tensor(zr[:, 1:2], zr[:, 0:1], minus_half[:, :], ALU.pow).then_inc(po_z, 1)
                eng.wait_ge(po_z, q * 4 + (START + 2))
                eng.sem_inc(stood, 1)
                eng.tensor_scalar(zr[:, 2:3], zr[:, 1:2], 0.5, None, ALU.mult).then_inc(po_z, 1)
                eng.wait_ge(po_z, q * 4 + (START + 3))
                eng.sem_inc(stood, 1)
                eng.tensor_scalar(zr[:, 3:4], zmv[:, 0:1], zr[:, 2:3], -1.0, ALU.mult, ALU.mult).then_inc(po_z, 1)

            def silu_z(st, j):
                q = j + Q * st
                eng.wait_ge(ac_z, q * 2 + (START + 2))
                eng.tensor_tensor(zt[:, :], zt[:, :], zh[:, :], ALU.mult).then_inc(po_sz, 1)
                eng.wait_ge(po_sz, q * 2 + (START + 1))
                eng.tensor_tensor(zh[:, :], zh[:, :], zt[:, :], ALU.add).then_inc(po_sz, 1)

            def times_u(st, j):
                b, q = st + 1, j + Q * (st + 1)
                eng.wait_ge(ve_dl, q + (START + 1))
                eng.wait_ge(ve_u, q + (START + 1))
                if b >= 2:
                    eng.wait_ge(po_dbu, NS * (b - 1) + START)
                eng.tensor_tensor(du[:, b % 2, bass.ds(j, 1), :], delta[:, b % 2, bass.ds(j, 1), :],
                                  u[:, bass.ds(j, 1), :], ALU.mult).then_inc(po_du, 1)

            def y_times_z(st, j):
                b, f = st - 1, j + Q * (st - 1)
                eng.wait_ge(ve_f, f * 3 + START)
                block_b = lambda t, depth: t[:, b % depth, bass.ds(j, 1), :].rearrange("p a l -> p (a l)")
                eng.tensor_tensor(fm[:, :], block_b(acc, 3), block_b(sz_t, 2), ALU.mult).then_inc(yz_made, 1)

            for e in range(Q // 2):
                times_u(-1, e)
            for run in RUNS:
                st = run[0]
                if run[1] == 0:
                    eng.wait_ge(po_du, START + Q * (st + 1))
                with each_turn(eng, run) as j:
                    times_b(st, j, 0, slice(0, Q) if run[1] or not st else slice(Q - 1, Q))
                    if ffn_in(st) and run[1] > 0:
                        y_times_z(st, j)
                    if prepare_in(st) and run[1] > 0:
                        times_u(st, j - 1)
                    times_b(st, j, 1)
                    if ffn_in(st):
                        scale_of_f(st, j)
                    scale_of_z(st, j)
                    times_b(st, j, 2)
                    times_b(st, j, 3)
                    silu_z(st, j)
                if prepare_in(st) and run[2] == Q:
                    eng.wait_ge(po_du, START + Q * (st + 1) + Q - 1)
                    times_b(st + 1, 0, 0, slice(0, Q - 1))
                    times_u(st, Q - 1)

            for t in range(Q):
                eng.wait_ge(cl_res[t], 4)
                fr_t = fr_close(t)
                eng.tensor_tensor(fr_t[:, 0:1], mv_close(t)[:, 1:2], eps_c[:, :], ALU.add).then_inc(cl_scale[t], 1)
                eng.wait_ge(cl_scale[t], 1)
                eng.tensor_tensor(fr_t[:, 1:2], fr_t[:, 0:1], minus_half[:, :], ALU.pow).then_inc(cl_scale[t], 1)
                eng.wait_ge(cl_scale[t], 2)
                eng.tensor_scalar(fr_t[:, 2:3], mv_close(t)[:, 0:1], fr_t[:, 1:2], -1.0, ALU.mult,
                                  ALU.mult).then_inc(cl_scale[t], 1)

        @block.tensor
        def _(eng):
            started(eng, [pe_in, pe_dl, pe_turn, pe_st, pe_sc, pe_hu, pe_x2, pe_v])

            def in_projection(st, j, k):
                b, q = st + 2, j + Q * (st + 2)
                if k == 0:
                    eng.wait_ge(s_cx[b % 2], 16 * (b // 2 + 1))
                    eng.wait_ge(s_win, (q - 2 * Q + 1) * 16)
                    eng.wait_ge(ve_tap, q * 3 + START)
                    eng.wait_ge(ve_dl, q + (START - Q))
                mm = eng.matmul(p_pr[:, :], w_in[:, k, :], cx[:, b % 2, k, :], start=(k == 0), stop=(k == KD - 1))
                if k == KD - 1:
                    mm.then_inc(pe_in, 1)

            def in_projection_open(b, e):
                eng.wait_ge(s_cx[b], 16)
                for k in range(KD):
                    mm = eng.matmul(banks_open[b][e], w_in_all[:, k, e * P:(e + 1) * P], cx[:, b, k, :],
                                    start=(k == 0), stop=(k == KD - 1))
                mm.then_inc(pe_in, 1)

            def small_projection(b, uses, blocks=range(Q)):
                if 0 in blocks:
                    eng.wait_ge(ac_turn, START + uses)
                for k in blocks:
                    eng.wait_ge(ve_u, START + Q * b + k + 1)
                    mm = eng.matmul(p_rows[0:BROW + 2 * NS, :], w_small[:, k, :], u[:, k, :], start=(k == 0), stop=(k == Q - 1))
                if k == Q - 1:
                    mm.then_inc(pe_turn, 1)

            def turn_c(uses):
                eng.wait_ge(ac_turn, START + uses)
                for t in range(Q):
                    mm = eng.transpose(p_tr[:, t, 0:2 * NS], bc[:, t * P:(t + 1) * P], ident[0:2 * NS, 0:2 * NS])
                mm.then_inc(pe_turn, 1)

            def dt_projection(st, j):
                b, q = st + 1, j + Q * (st + 1)
                eng.wait_ge(s_wdt, (q - Q + 1) * 32)
                eng.wait_ge(ac_xd, START + b + 1)
                if project_in(st):
                    eng.wait_ge(ve_tap, q * 3 + (START + 3 * Q + 3))
                else:
                    eng.wait_ge(ve_dl, q + START)
                eng.matmul(p_pr[:, :], w_dt[:, :], xd[:, :], start=True, stop=True).then_inc(pe_dl, 1)

            def turn_four(source, uses):
                eng.wait_ge(ac_turn, uses + START)
                for k in range(Q):
                    mm = eng.transpose(p_tr[:, k, :], source[:, k * P:(k + 1) * P], ident[:, :])
                mm.then_inc(pe_turn, 1)

            def turn_states(st, j, i, t):
                n = j * NB + NS * st + i
                if t == 0:
                    eng.wait_ge(ve_scan, n * Q + (START + Q))
                eng.wait_ge(ve_acc, n * Q + (START + t - 1))
                for k in range(Q):
                    mm = eng.transpose(p_st[:, t % 2, k * P:(k + 1) * P], state[:, i % 2, k, t * P:(t + 1) * P],
                                       ident[:, :])
                mm.then_inc(pe_st, 1)

            def scores(run, j):
                f = j + Q * (run[0] - 1)
                eng.wait_ge(ac_turn, turn(run, j, "h") + (START + 1))
                eng.wait_ge(ac_out, f + START)
                for k in range(Q):
                    mm = eng.matmul(p_f[:, 0:S], h_t[:, k, :], router[:, k, :], start=(k == 0), stop=(k == Q - 1))
                mm.then_inc(pe_sc, 1)

            def times_u_weights(st, j, k):
                if k == 0:
                    eng.wait_ge(ac_sc, (j + Q * (st - 1)) + (START + 1))
                mm = eng.matmul(p_f[:, :], h_t[:, k, :], u_sb[:, k, :], start=(k == 0), stop=(k == Q - 1))
                if k == Q - 1:
                    mm.then_inc(pe_hu, 1)

            def turn_gated(run, j):
                eng.wait_ge(ve_hug, (j + Q * (run[0] - 1)) + (START + 1))
                eng.matmul(p_f[:, :], ident[:, :], x2[:, :], start=True, stop=False).then_inc(pe_x2, 1)
                turn_four(hug[:, :, :].rearrange("p s r -> p (s r)"), turn(run, j, "hug"))

            def times_v(j, run):
                f = j + (Q * (run[0] - 1) - 1)
                eng.wait_ge(ac_turn, turn(run, j, None) + START)
                for k in range(Q):
                    mm = eng.matmul(p_f[:, :], hug_t[:, k, :], v_sb[:, k, :], start=False, stop=(k == Q - 1))
                mm.then_inc(pe_v, 1)

            eng.wait_ge(s_first, 16)
            in_projection_open(0, 0)
            eng.wait_ge(s_rest, 16)
            for e in range(1, Q):
                in_projection_open(0, e)
            for e in range(Q - 1):
                in_projection_open(1, e)
            eng.wait_ge(s_second, 16 * 6)
            eng.wait_ge(po_c, 7)
            small_projection(0, 0)
            eng.wait_ge(ac_xd, START + 1)
            for e in range(Q):
                eng.wait_ge(ve_tap, START + 3 * (e + 1))
                eng.matmul(p_scan[:, e, :], w_dt_all[:, e * P:(e + 1) * P], xd[:, :], start=True, stop=True).then_inc(pe_dl, 1)
            eng.wait_ge(ve_tap, START + 3 * Q + 3)
            in_projection_open(1, 3)
            for e in range(Q):
                eng.wait_ge(ac_du, START + e + 1)
                turn_four(dut_open[:, e, :], 1 + e)
            turn_c(1 + Q)
            eng.wait_ge(s_w, 16 * N_W)
            eng.wait_ge(ve_c, 3)
            eng.wait_ge(ve_tap, START + 3 * Q + 9)
            eng.matmul(p_f[:, 0:S], wa_wide[:, :], at_sb[:, :], start=True, stop=True).then_inc(pe_c, 1)

            for run in RUNS:
                st = run[0]
                if st == 1 and run[1] == 0:
                    eng.wait_ge(s_uv, 32)
                    eng.wait_ge(ac_c, 4)
                with each_turn(eng, run) as j:
                    after = {}
                    if ffn_end_in(st, run[1]):
                        times_v(j, run)
                    if project_in(st):
                        in_projection(st, j, 0)
                        if ffn_in(st):
                            after[0, 1] = [lambda: in_projection(st, j, 1)]
                        else:
                            in_projection(st, j, 1)
                    small = prepare_in(st) and run[1] == 0

                    def put(at, *steps):
                        after.setdefault(at, []).extend(steps)

                    if small:
                        for k in range(Q):
                            put((0, k), lambda k=k: small_projection(st + 1, turn(run, j, "small"), [k]))
                    if ffn_in(st):
                        put((1, 1) if small else (0, 3),
                            lambda: eng.wait_ge(ac_h, (j + Q * (st - 1)) + (START + 1)),
                            lambda: turn_four(h, turn(run, j, "h")))
                        put((1, 3) if small else (1, 1), lambda: scores(run, j))
                        for k in range(Q):
                            put([(2, 2), (2, 3), (3, 0), (3, 1)][k], lambda k=k: times_u_weights(st, j, k))
                    if prepare_in(st):
                        put((2, 0),
                            lambda: eng.wait_ge(ac_du, (j + Q * (st + 1)) + (START + 1)),
                            lambda: turn_four(dut, turn(run, j, "du")))
                        put((1, 2), lambda: dt_projection(st, j))
                        if small:
                            put((2, 1), lambda: turn_c(turn(run, j, "c")))
                    put((3, 1),
                        lambda: eng.wait_ge(po_sz, (j + Q * st) * 2 + (START + 2)),
                        lambda: turn_four(zh, turn(run, j, "z")))
                    if ffn_in(st):
                        put((3, 3), lambda: turn_gated(run, j))
                    for i in range(NB):
                        for t in range(Q):
                            if scan_in(st):
                                turn_states(st, j, i, t)
                            for step in after.get((i, t), []):
                                step()

            times_v(0, CLOSING)

            def turn_h_close(t):
                if t == 0:
                    eng.wait_ge(ve_acc, START + Q * NS * B)
                if t >= 2:
                    eng.wait_ge(cl_h_copied, t - 1)
                eng.wait_ge(cl_h, t + 1)
                for k in range(Q):
                    mm = eng.transpose(close_turn[t % 2][:, k * P:(k + 1) * P], h_close[:, t, k * P:(k + 1) * P], ident[:, :])
                mm.then_inc(cl_pe_h, 1)

            def scores_close(t):
                if t == 1:
                    eng.wait_ge(ac_out, START + Q * (B - 1))
                if t >= 2:
                    eng.wait_ge(cl_sc_copied, t - 1)
                eng.wait_ge(cl_h_copied, t + 1)
                for k in range(Q):
                    mm = eng.matmul(close_scores[t % 2][:, 0:S], ht_close[:, t, k * P:(k + 1) * P], router[:, k, :],
                                    start=(k == 0), stop=(k == Q - 1))
                mm.then_inc(cl_sc, 1)

            def times_u_close(t):
                for k in range(Q):
                    mm = eng.matmul(p_scan[:, t, :], ht_close[:, t, k * P:(k + 1) * P], u_sb[:, k, :],
                                    start=(k == 0), stop=(k == Q - 1))
                mm.then_inc(cl_hu, 1)

            def turn_gated_close(t):
                eng.wait_ge(cl_hug, t + 1)
                if t == 0:
                    eng.wait_ge(cl_h_copied, Q)
                if t >= 2:
                    eng.wait_ge(cl_hug_copied, t - 1)
                for k in range(Q):
                    mm = eng.transpose(close_turn[t % 2][:, k * P:(k + 1) * P], hug_close[:, t, k * P:(k + 1) * P], ident[:, :])
                mm.then_inc(cl_pe_hug, 1)

            def times_v_close(t):
                eng.wait_ge(cl_hug_copied, t + 1)
                for k in range(Q):
                    mm = eng.matmul(p_scan[:, t, :], hugt_close[:, t, k * P:(k + 1) * P], v_sb[:, k, :],
                                    start=(k == 0), stop=(k == Q - 1))
                mm.then_inc(cl_v, 1)

            turn_h_close(0)
            for t in range(Q):
                if t < Q - 1:
                    turn_h_close(t + 1)
                scores_close(t)
                if t == Q - 1:
                    turn_gated_close(0)
                    turn_gated_close(1)
                times_u_close(t)
            times_v_close(0)
            times_v_close(1)
            turn_gated_close(2)
            turn_gated_close(3)
            times_v_close(2)
            times_v_close(3)

        @block.scalar
        def _(eng):
            started(eng, [ac_v, ac_th, ac_xd, ac_sp, ac_du, ac_z, ac_turn, ac_da, ac_h, ac_sc, ac_e, ac_out, s_out])
            def exp_table():
                eng.activation(table[:, :], minus_half[:, :], ACT.Exp)

            def conv_first(st, j):
                q = j + Q * (st + 2)
                eng.wait_ge(pe_in, q + (START + 1))
                eng.wait_ge(ve_u, q + START)
                eng.activation(v[:, :], p_pr[:, :], ACT.Identity, bias=cb[:, bass.ds(j, 1)],
                               scale=cw[:, bass.ds(j, 1), TAPS - 1:TAPS].rearrange("p a b -> p (a b)")).then_inc(ac_v, 1)

            def tanh_v(st, j):
                q = j + Q * (st + 2)
                eng.wait_ge(ve_tap, q * 3 + (START + 3))
                eng.activation(th[:, :], v[:, :], ACT.Tanh).then_inc(ac_th, 1)

            def copy_small(b, uses):
                eng.wait_ge(pe_turn, START + uses + 1)
                eng.wait_ge(pe_dl, START + Q * b)
                eng.activation(xd[0:DR, :], p_rows[0:DR, :], ACT.Copy).then_inc(ac_xd, 1)
                if b:
                    eng.wait_ge(s_bst, 16 * b)
                eng.activation(bc[:, :], p_rows[BROW:BROW + 2 * NS, :], ACT.Copy).then_inc(ac_turn, 1)

            def copy_c(b, uses):
                eng.wait_ge(pe_turn, START + uses + 1)
                if b >= 2:
                    eng.wait_ge(ve_acc, START + Q * NS * (b - 1))
                eng.activation(c_t[:, b % 2, :, :], p_tr[:, :, NS:2 * NS], ACT.Copy).then_inc(ac_turn, 1)

            def softplus_tail(st, j, part):
                q = j + Q * (st + 1)
                if part == 0:
                    eng.wait_ge(pe_dl, q + (START + 1))
                    eng.wait_ge(ve_dl, q + START)
                    eng.activation(sp[:, :], p_pr[:, :], ACT.Abs).then_inc(ac_sp, 1)
                    eng.wait_ge(ac_sp, q * 3 + (START + 1))
                    eng.activation(sp[:, :], sp[:, :], ACT.Exp, scale=-1.0).then_inc(ac_sp, 1)
                else:
                    eng.wait_ge(ac_sp, q * 3 + (START + 2))
                    eng.activation(sp[:, :], sp[:, :], ACT.Ln, bias=1.0).then_inc(ac_sp, 1)

            def skip(st, j):
                q = j + Q * (st + 1)
                eng.wait_ge(ve_u, q + (START + 1))
                eng.activation(dut[:, :], u[:, bass.ds(j, 1), :].rearrange("p a l -> p (a l)"), ACT.Copy,
                               scale=dsk[:, bass.ds(j, 1)]).then_inc(ac_du, 1)

            def z_half(st, j, part):
                b, q = st, j + Q * st
                if part == 0:
                    eng.wait_ge(s_x[b % 3], 16 * (b // 3 + 1))
                    eng.wait_ge(po_z, q * 4 + (START + 4))
                    eng.wait_ge(po_sz, q * 2 + START)
                row = xs[:, b % 3, bass.ds(j, 1), :].rearrange("p a l -> p (a l)")
                eng.activation((zh, zt)[part][:, :], row, (ACT.Identity, ACT.Tanh)[part],
                               bias=zr[:, 3:4], scale=zr[:, 2:3]).then_inc(ac_z, 1)

            def copy_turn(dest, uses):
                eng.wait_ge(pe_turn, uses + (START + 1))
                eng.activation(dest, p_tr[:, :, :], ACT.Copy).then_inc(ac_turn, 1)

            def decay(st, j, i, k):
                b, m = st, i * Q + k
                eng.wait_ge(ve_scan, (j * NB + NS * st) * Q + (START + 1 + m - DA_AGO[m]))
                eng.activation(p_da[:, DA_BANK[m], :], delta[:, b % 2, k, :], ACT.Exp,
                               scale=a_neg[:, k, bass.ds(j * NB + i, 1)]).then_inc(ac_da, 1)

            def normed(st, j):
                f = j + Q * (st - 1)
                eng.wait_ge(po_f, f * 3 + (START + 3))
                eng.activation(h[:, :], x2[:, :], ACT.Identity, bias=fr[:, 2:3], scale=fr[:, 1:2]).then_inc(ac_h, 1)

            def copy_scores(st, j):
                f = j + Q * (st - 1)
                eng.wait_ge(pe_sc, f + (START + 1))
                eng.wait_ge(ve_g, f * 9 + START)
                eng.activation(sc[:, :], p_f[:, 0:S], ACT.Copy).then_inc(ac_sc, 1)

            def exp_scores(st, j):
                f = j + Q * (st - 1)
                eng.wait_ge(ve_top, f * 4 + (START + 2))
                eng.activation(ex[:, :], sc[:, :], ACT.Exp, bias=nmx[:, :], accum_out=z_sum[:, :]).then_inc(ac_e, 1)

            def copy_out(st, j):
                f = j + (Q * (st - 1) - 1)
                eng.wait_ge(pe_v, f + (START + 1))
                eng.wait_ge(s_out, f * 16 + START)
                eng.activation(ot[:, :], p_f[:, :], ACT.Copy).then_inc(ac_out, 1)
                eng.wait_ge(ac_out, f + (START + 1))
                eng.dma_start(out_rows[bass.ds(f * P, P), :], ot[:, :]).then_inc(s_out, 16)

            def conv_first_open(b, e):
                eng.wait_ge(pe_in, START + Q * b + e + 1)
                eng.activation(v_open[b][:, e, :], banks_open[b][e], ACT.Identity, bias=cb[:, e:e + 1],
                               scale=cw[:, e, TAPS - 1:TAPS]).then_inc(ac_v, 1)

            def tanh_open(b, e):
                eng.wait_ge(ve_tap, START + 3 * (Q * b + e + 1))
                eng.activation(th_open[b][:, e, :], v_open[b][:, e, :], ACT.Tanh).then_inc(ac_th, 1)

            eng.wait_ge(po_c, 5)
            exp_table()
            eng.wait_ge(ve_c, 2)
            conv_first_open(0, 0)
            for e in range(1, Q):
                conv_first_open(0, e)
                tanh_open(0, e - 1)
            tanh_open(0, Q - 1)
            conv_first_open(1, 0)
            eng.wait_ge(po_c, 7)
            copy_small(0, 0)
            conv_first_open(1, 1)
            conv_first_open(1, 2)
            eng.wait_ge(s_second, 16 * 6)
            halves = [slice(0, Q // 2), slice(Q // 2, Q)]
            for i, half in enumerate(halves):
                eng.wait_ge(pe_dl, START + half.stop)
                eng.activation(sp_open[:, half, :], p_scan[:, half, :], ACT.Abs).then_inc(ac_sp, 2)
                eng.wait_ge(ac_sp, START + 4 * i + 2)
                eng.activation(sp_open[:, half, :], sp_open[:, half, :], ACT.Exp, scale=-1.0).then_inc(ac_sp, 2)
            eng.activation(a_neg[:, :, :], a_neg[:, :, :], ACT.Exp).then_inc(ac_c, 1)
            for i, half in enumerate(halves):
                eng.wait_ge(ac_sp, START + 4 * (i + 1))
                eng.activation(sp_open[:, half, :], sp_open[:, half, :], ACT.Ln, bias=1.0).then_inc(ac_sp, 2)
            conv_first_open(1, 3)

            def skip_open(e):
                eng.wait_ge(ve_u, START + e + 1)
                eng.activation(dut_open[:, e, :], u[:, e, :], ACT.Copy, scale=dsk[:, e:e + 1]).then_inc(ac_du, 1)

            skip_open(0)
            for e in range(Q):
                if e < Q - 1:
                    skip_open(e + 1)
                copy_turn(acc[:, 0, :, e * P:(e + 1) * P], 1 + e)
            copy_c(0, 1 + Q)
            tanh_open(1, 0)
            tanh_open(1, 1)
            eng.wait_ge(ve_c, 4)

            for run in RUNS:
                st = run[0]
                if scan_in(st) and run[1] == 0:
                    eng.wait_ge(ve_dl, START + Q * (st + 1))
                with each_turn(eng, run) as j:
                    after = {}
                    small = prepare_in(st) and run[1] == 0

                    def put(at, step):
                        after.setdefault(at, []).append(step)

                    if run == (0, 0, 1):
                        put((0, 0), lambda: tanh_open(1, 2))
                        put((0, 1), lambda: tanh_open(1, 3))

                    def copy_h():
                        eng.wait_ge(pe_hu, (j + Q * (st - 1)) + START)
                        copy_turn(h_t[:, :, :], turn(run, j, "h"))

                    def copy_du():
                        b = st + 1
                        if b == 1:
                            eng.wait_ge(ve_u, START + 2 * Q)
                        if b >= 3:
                            eng.wait_ge(ve_f, START + 3 * Q * (b - 2))
                        copy_turn(acc[:, b % 3, :, bass.ds(j * P, P)], turn(run, j, "du"))

                    def copy_z():
                        if st >= 2:
                            eng.wait_ge(ve_f, START + 3 * Q * (st - 1))
                        copy_turn(sz_t[:, st % 2, :, bass.ds(j * P, P)], turn(run, j, "z"))

                    def copy_gated():
                        f = j + Q * (st - 1)
                        eng.wait_ge(pe_v, f + START)
                        copy_turn(hug_t[:, :, :], turn(run, j, "hug"))

                    if prepare_in(st) and run[1] == 0:
                        put((2, 0), lambda: copy_small(st + 1, turn(run, j, "small")))
                    if ffn_end_in(st, run[1]):
                        put((1, 0), lambda: copy_out(st, j))
                    if ffn_in(st):
                        put((1, 1), lambda: normed(st, j))
                        put((2, 3) if small else (2, 2), copy_h)
                        put((3, 1) if small else (3, 0), lambda: copy_scores(st, j))
                    if project_in(st):
                        put((1, 3), lambda: conv_first(st, j))
                    if prepare_in(st):
                        put((0, 2), lambda: skip(st, j))
                        put((3, 2) if small else (3, 1), copy_du)
                    if scan_in(st):
                        put((2, 0), lambda: z_half(st, j, 0))
                        put((2, 3), lambda: z_half(st, j, 1))
                    if prepare_in(st):
                        put((3, 2), lambda: softplus_tail(st, j, 0))
                    if prepare_in(st) and run[1] == 0:
                        put((3, 2), lambda: copy_c(st + 1, turn(run, j, "c")))
                    if ffn_in(st):
                        put((3, 3), lambda: exp_scores(st, j))
                    if project_in(st):
                        put((3, 3), lambda: tanh_v(st, j))
                    if prepare_in(st):
                        put((3, 3), lambda: softplus_tail(st, j, 1))
                    if prepare_in(st):
                        put((3, 3), exp_table)
                    put((3, 3), copy_z)
                    if ffn_in(st):
                        put((3, 3), copy_gated)
                    for i in range(NB):
                        for k in range(Q):
                            if scan_in(st):
                                decay(st, j, i, k)
                            for step in after.get((i, k), []):
                                step()
                if run == (0, 0, 1):
                    eng.wait_ge(s_w, 16 * N_W)
                    eng.activation(gx[:, :], gx[:, :], ACT.Tanh).then_inc(ac_c, 1)
                    eng.activation(gf[:, :], gf[:, :], ACT.Tanh).then_inc(ac_c, 1)
                    eng.wait_ge(pe_c, 1)
                    eng.activation(aw[:, :], p_f[:, 0:S], ACT.Exp, scale=-1.0).then_inc(ac_c, 1)
            def normed_close(t):
                eng.wait_ge(cl_scale[t], 3)
                eng.activation(h_close[:, t, :], x2_close[:, t, :], ACT.Identity, bias=fr_close(t)[:, 2:3],
                               scale=fr_close(t)[:, 1:2]).then_inc(cl_h, 1)

            def copy_h_close(t):
                eng.wait_ge(cl_pe_h, t + 1)
                eng.activation(ht_close[:, t, :], close_turn[t % 2], ACT.Copy).then_inc(cl_h_copied, 1)

            def copy_scores_close(t):
                eng.wait_ge(cl_sc, t + 1)
                eng.activation(wide_close(t, SC), close_scores[t % 2][:, 0:S], ACT.Copy).then_inc(cl_sc_copied, 1)

            def exp_scores_close(t):
                eng.wait_ge(cl_top[t], 2)
                eng.activation(wide_close(t, EX), wide_close(t, SC), ACT.Exp, bias=nmx_close(t),
                               accum_out=sum_close(t)).then_inc(cl_ex, 1)

            def copy_gated_close(t):
                eng.wait_ge(cl_pe_hug, t + 1)
                eng.activation(hugt_close[:, t, :], close_turn[t % 2], ACT.Copy).then_inc(cl_hug_copied, 1)

            normed_close(0)
            copy_out(B, 0)
            for t in range(Q):
                if t < Q - 1:
                    normed_close(t + 1)
                copy_h_close(t)
                if t:
                    copy_scores_close(t - 1)
                if t == 2:
                    exp_scores_close(0)
                    exp_scores_close(1)
            copy_scores_close(Q - 1)
            copy_gated_close(0)
            copy_gated_close(1)
            exp_scores_close(2)
            exp_scores_close(3)
            copy_gated_close(2)
            copy_gated_close(3)
            eng.wait_ge(s_out, START + 16 * Q * (B - 1))

        @block.vector
        def _(eng):
            started(eng, [ve_tap, ve_u, ve_dl, ve_zs, ve_scan, ve_acc, ve_f, ve_top, ve_g, ve_hug])
            eng.wait_ge(s_conv, 32)
            eng.tensor_scalar(cw[:, :, :], cw[:, :, :], 0.5, None, ALU.mult).then_inc(ve_c, 1)
            eng.tensor_scalar(cb[:, :], cb[:, :], 0.5, None, ALU.mult).then_inc(ve_c, 1)
            eng.wait_ge(ve_c, 2)

            def taps(q, j, v, bank, which=range(1, TAPS)):
                if 1 in which:
                    eng.wait_ge(ac_v, q + (START + 1))
                for s in which:
                    if s > 1:
                        eng.wait_ge(ve_tap, q * 3 + (START + s - 1))
                    eng.scalar_tensor_tensor(
                        out=v[:, s:], in0=bank[:, 0:L - s], in1=v[:, s:], op0=ALU.mult, op1=ALU.add,
                        scalar=cw[:, bass.ds(j, 1), TAPS - 1 - s:TAPS - s].rearrange("p a b -> p (a b)"),
                    ).then_inc(ve_tap, 1)

            def silu_u(b, j, v, th):
                q = j + Q * b
                eng.wait_ge(ac_th, q + (START + 1))
                if b:
                    eng.wait_ge(pe_turn, START + (turns_before((b - 2, 0, 1)) if b > 1 else 0) + 1)
                    eng.wait_ge(po_du, q + (START - Q + 1))
                    eng.wait_ge(ac_du, q + (START - Q + 1))
                eng.scalar_tensor_tensor(out=u[:, bass.ds(j, 1), :].rearrange("p a l -> p (a l)"), in0=th,
                                         scalar=1.0, in1=v, op0=ALU.add, op1=ALU.mult).then_inc(ve_u, 1)

            def softplus(st, j):
                b, q = st + 1, j + Q * (st + 1)
                eng.wait_ge(ac_sp, q * 3 + (START + 3))
                if b >= 2:
                    eng.wait_ge(ac_da, START + Q * NS * (b - 1))
                    eng.wait_ge(po_du, START + Q * (b - 1))
                eng.scalar_tensor_tensor(out=delta[:, b % 2, bass.ds(j, 1), :].rearrange("p a l -> p (a l)"),
                                         in0=p_pr[:, :], scalar=0.0, in1=sp[:, :], op0=ALU.max,
                                         op1=ALU.add).then_inc(ve_dl, 1)

            def z_statistics(st, j, part):
                b, q = st, j + Q * st
                if part == 0:
                    eng.wait_ge(s_x[b % 3], 16 * (b // 3 + 1))
                    eng.wait_ge(ve_zs, q * 2 + START)
                    eng.bn_stats(zst[:, :], xs[:, b % 3, bass.ds(j, 1), :].rearrange("p a l -> p (a l)")).then_inc(ve_zs, 1)
                else:
                    eng.wait_ge(ve_zs, q * 2 + (START + 1))
                    eng.wait_ge(po_z, q * 4 + START)
                    eng.sem_inc(stood, 1)
                    eng.bn_aggr(zmv[:, :], zst[:, :]).then_inc(ve_zs, 1)

            def scan(st, j, i, k):
                n = j * NB + NS * st + i
                if k == 0:
                    eng.wait_ge(po_dbu, n + (START + 1))
                    eng.wait_ge(pe_st, (n - 1) * Q + START)
                eng.wait_ge(ac_da, n * Q + (START + k + 1))
                eng.tensor_tensor_scan(state[:, i % 2, k, :], p_da[:, DA_BANK[i * Q + k], :], dbu[:, i % 2, k, :], 0.0,
                                       ALU.mult, ALU.add).then_inc(ve_scan, 1)

            def accumulate(st, j, i, t):
                b, n = st, j * NB + NS * st + i
                eng.wait_ge(pe_st, n * Q + (START + t + 1))
                eng.wait_ge(ve_acc, n * Q + (START + t - Q + 1))
                eng.scalar_tensor_tensor(out=acc[:, b % 3, t, :], in0=p_st[:, t % 2, :],
                                         scalar=c_t[:, b % 2, t, bass.ds(j * NB + i, 1)], in1=acc[:, b % 3, t, :],
                                         op0=ALU.mult, op1=ALU.add).then_inc(ve_acc, 1)

            def residual(st, j, meanwhile):
                b, f = st - 1, j + Q * (st - 1)
                if isinstance(j, int):
                    eng.tensor_tensor(fm[:, :], acc[:, b % 3, j, :], sz_t[:, b % 2, j, :], ALU.mult).then_inc(yz_made, 1)
                for step in meanwhile[:-1]:
                    step()
                eng.wait_ge(yz_made, f + (START + 1))
                eng.wait_ge(ac_h, f + START)
                eng.wait_ge(pe_x2, f + START)
                eng.scalar_tensor_tensor(out=x2[:, :], in0=fm[:, :], scalar=gx[:, :],
                                         in1=xs[:, b % 3, bass.ds(j, 1), :].rearrange("p a l -> p (a l)"),
                                         op0=ALU.mult, op1=ALU.add).then_inc(ve_f, 1)
                for step in meanwhile[-1:]:
                    step()
                eng.wait_ge(ve_f, f * 3 + (START + 1))
                eng.bn_stats(fst[:, :], x2[:, :]).then_inc(ve_f, 1)

            def residual_statistics(st, j):
                f = j + Q * (st - 1)
                eng.wait_ge(ve_f, f * 3 + (START + 2))
                eng.wait_ge(po_f, f * 3 + START)
                eng.sem_inc(stood, 1)
                eng.bn_aggr(fmv[:, :], fst[:, :]).then_inc(ve_f, 1)

            def best_two(st, j, part):
                f = j + Q * (st - 1)
                if part == 0:
                    eng.wait_ge(ac_sc, f + (START + 1))
                    eng.wait_ge(ve_g, f * 9 + START)
                    eng.sem_inc(stood, 1)
                    eng.max(top[:, :], sc[:, :]).then_inc(ve_top, 1)
                elif part == 1:
                    eng.wait_ge(ve_top, f * 4 + (START + 1))
                    eng.wait_ge(ac_e, f + START)
                    eng.tensor_scalar(nmx[:, :], top[:, 0:1], -1.0, None, ALU.mult).then_inc(ve_top, 1)
                    eng.max_index(top_i[:, :], top[:, :], sc[:, :]).then_inc(ve_top, 1)
                else:
                    eng.wait_ge(ve_top, f * 4 + (START + 3))
                    eng.tensor_copy(top_f[:, :], top_i[:, 0:2]).then_inc(ve_top, 1)

            def gates(st, j, meanwhile):
                f = j + Q * (st - 1)
                made = lambda n: eng.wait_ge(ve_g, f * 9 + (START + n))
                eng.wait_ge(ac_e, f + (START + 1))
                eng.wait_ge(ve_top, f * 4 + (START + 4))
                eng.wait_ge(ve_hug, f + START)
                eng.scalar_tensor_tensor(out=e1[:, :], in0=iota_f[:, :], scalar=top_f[:, 0:1], in1=ex[:, :],
                                         op0=ALU.is_equal, op1=ALU.mult).then_inc(ve_g, 1)
                eng.scalar_tensor_tensor(out=e2[:, :], in0=iota_f[:, :], scalar=top_f[:, 1:2], in1=ex[:, :],
                                         op0=ALU.is_equal, op1=ALU.mult).then_inc(ve_g, 1)
                made(2)
                eng.scalar_tensor_tensor(out=em[:, :], in0=e1[:, :], scalar=1.0, in1=e2[:, :], op0=ALU.mult,
                                         op1=ALU.add, accum_out=ga[:, 0:1]).then_inc(ve_g, 1)
                made(3)
                eng.scalar_tensor_tensor(out=ga[:, 1:2], in0=z_sum[:, :], scalar=GATE_EPS, in1=ga[:, 0:1],
                                         op0=ALU.mult, op1=ALU.add).then_inc(ve_g, 1)
                eng.scalar_tensor_tensor(out=gsc[:, :], in0=em[:, :], scalar=1.0, in1=aw[:, :], op0=ALU.mult,
                                         op1=ALU.mult, accum_out=ga[:, 3:4]).then_inc(ve_g, 1)
                for step in meanwhile[0:1]:
                    step()
                made(5)
                eng.reciprocal(ga[:, 2:3], ga[:, 1:2]).then_inc(ve_g, 1)
                for step in meanwhile[1:2]:
                    step()
                made(6)
                eng.tensor_scalar(ga[:, 4:5], ga[:, 3:4], ga[:, 2:3], 0.2, ALU.mult, ALU.mult).then_inc(ve_g, 1)
                made(7)
                eng.tensor_scalar(ga[:, 5:6], ga[:, 4:5], 0.9, ga[:, 2:3], ALU.add, ALU.mult).then_inc(ve_g, 1)
                for step in meanwhile[2:]:
                    step()
                made(8)
                eng.tensor_scalar(gw[:, :], em[:, :], ga[:, 5:6], gf[:, :], ALU.mult, ALU.mult).then_inc(ve_g, 1)
                made(9)
                eng.wait_ge(pe_hu, f + (START + 1))
                eng.tensor_tensor(hug[:, :, :], p_f[:, :].rearrange("p (s r) -> p s r", r=R),
                                  gw[:, :].unsqueeze(2).to_broadcast([P, S, R]), ALU.mult).then_inc(ve_hug, 1)

            def taps_open(b, e):
                taps(Q * b + e, e, v_open[b][:, e, :], banks_open[b][e])

            def silu_u_open(b, e):
                silu_u(b, e, v_open[b][:, e, :], th_open[b][:, e, :])

            taps_open(0, 0)
            for e in range(1, Q):
                taps_open(0, e)
                silu_u_open(0, e - 1)
            silu_u_open(0, Q - 1)
            taps_open(1, 0)
            taps_open(1, 1)
            eng.wait_ge(s_w, 16 * N_W)
            eng.wait_ge(po_c, 7)
            eng.tensor_copy(wa_wide[:, :], wa_sb[:, :].to_broadcast([AD, P])).then_inc(ve_c, 1)
            eng.wait_ge(ac_c, 1)
            eng.tensor_scalar(a_neg[:, :, :], a_neg[:, :, :], -1.0, None, ALU.mult).then_inc(ve_c, 1)
            eng.tensor_copy(iota_f[:, :], iota_i[:, :]).then_inc(ve_c, 1)
            for i, half in enumerate([slice(0, Q // 2), slice(Q // 2, Q)]):
                eng.wait_ge(ac_sp, START + 10 + 2 * i)
                eng.scalar_tensor_tensor(out=delta[:, 0, half, :], in0=p_scan[:, half, :], scalar=0.0,
                                         in1=sp_open[:, half, :], op0=ALU.max, op1=ALU.add).then_inc(ve_dl, 2)
            for e in range(Q // 2, Q):
                eng.wait_ge(ve_dl, START + Q)
                eng.wait_ge(ve_u, START + e + 1)
                eng.tensor_tensor(du[:, 0, e, :], delta[:, 0, e, :], u[:, e, :], ALU.mult).then_inc(po_du, 1)
            taps_open(1, 2)
            taps_open(1, 3)
            eng.wait_ge(po_du, START + Q)

            for run in RUNS:
                st = run[0]
                if (scan_in(st) or ffn_in(st)) and run[1] == 0:
                    eng.wait_ge(ac_turn, START + turns_before((st, 0, 1)) - ffn_in(st - 1))
                if st == 1 and run[1] == 0:
                    eng.wait_ge(ac_c, 4)
                    eng.tensor_scalar(aw[:, :], aw[:, :], 1.0, None, ALU.add).then_inc(ve_c, 1)
                    eng.wait_ge(ve_c, 6)
                    eng.reciprocal(aw[:, :], aw[:, :]).then_inc(ve_c, 1)
                    eng.wait_ge(ve_c, 7)
                with each_turn(eng, run) as j:
                    between = {}

                    def put(at, step):
                        between.setdefault(at, []).append(step)

                    if run == (0, 0, 1):
                        for e in range(Q):
                            put((0, e), lambda e=e: silu_u_open(1, e))
                    if ffn_in(st):
                        put((0, 0), lambda: residual_statistics(st, j))
                    if project_in(st):
                        for s in range(1, TAPS):
                            put([(1, 2), (1, 3), (2, 0)][s - 1], lambda s=s: taps(j + Q * (st + 2), j, v[:, :], p_pr[:, :], [s]))
                        if run[1] > 0:
                            put((0, 3), lambda: silu_u(st + 2, j - 1, v[:, :], th[:, :]))
                    if ffn_in(st):
                        for part in range(3):
                            put((3, min(part + 1 + (prepare_in(st) and run[1] == 0), Q - 1)), lambda part=part: best_two(st, j, part))

                    statistics = [lambda part=part: z_statistics(st, j, part) for part in (0, 1)] if scan_in(st) else []
                    late = [lambda t=t: accumulate(st, j, -1, t) for t in range(2, Q)] if scan_in(st) and run[1] > 0 else []
                    if ffn_in(st):
                        residual(st, j, statistics[:1] + late + statistics[1:])
                        late = []
                        if not scan_in(st):
                            residual_statistics(st, j)
                    else:
                        for step in statistics:
                            step()
                    for i in range(NB):
                        for k in range(Q):
                            if scan_in(st):
                                scan(st, j, i, k)
                                if i:
                                    accumulate(st, j, i - 1, k)
                                elif k < len(late):
                                    late[k]()
                            for step in between.get((i, k), []):
                                step()
                    last = [lambda t=t: accumulate(st, j, NB - 1, t) for t in range(2)] if scan_in(st) else []
                    if prepare_in(st):
                        last.append(lambda: softplus(st, j))
                    if ffn_in(st):
                        gates(st, j, last)
                        last = []
                    for step in last:
                        step()
                if run[2] == Q and st < B - 1:
                    for t in range(2, Q):
                        accumulate(st, Q - 1, NB - 1, t)
                if project_in(st) and run[2] == Q:
                    silu_u(st + 2, Q - 1, v[:, :], th[:, :])

            def residual_close(t, part):
                last = B - 1
                if part:
                    eng.wait_ge(cl_res[t], part)
                elif t >= 2:
                    eng.wait_ge(ve_acc, START + Q * NS * B)
                if part == 0:
                    eng.tensor_tensor(fm_close[:, t, :], acc[:, last % 3, t, :], sz_t[:, last % 2, t, :],
                                      ALU.mult).then_inc(cl_res[t], 1)
                elif part == 1:
                    eng.scalar_tensor_tensor(out=x2_close[:, t, :], in0=fm_close[:, t, :], scalar=gx[:, :],
                                             in1=xs[:, last % 3, t, :], op0=ALU.mult, op1=ALU.add).then_inc(cl_res[t], 1)
                elif part == 2:
                    eng.bn_stats(stats_close(t), x2_close[:, t, :]).then_inc(cl_res[t], 1)
                else:
                    eng.bn_aggr(mv_close(t), stats_close(t)).then_inc(cl_res[t], 1)

            def top_two_close(t, part):
                if part == 0:
                    eng.wait_ge(cl_sc_copied, t + 1)
                    eng.max(top_close(t), wide_close(t, SC)).then_inc(cl_top[t], 1)
                elif part == 1:
                    eng.wait_ge(cl_top[t], 1)
                    eng.tensor_scalar(nmx_close(t), top_close(t)[:, 0:1], -1.0, None, ALU.mult).then_inc(cl_top[t], 1)
                elif part == 2:
                    eng.max_index(top_i_close[:, t, :], top_close(t), wide_close(t, SC)).then_inc(cl_top[t], 1)
                else:
                    eng.wait_ge(cl_top[t], 3)
                    eng.tensor_copy(topf_close(t), top_i_close[:, t, 0:2]).then_inc(cl_top[t], 1)

            def gates_close(t, part):
                ga_t, made = ga_close(t), cl_gate[t]
                e1_t, e2_t, em_t = wide_close(t, E1), wide_close(t, E2), wide_close(t, EM)
                if part == 0:
                    eng.wait_ge(cl_ex, t + 1)
                    eng.wait_ge(cl_top[t], 4)
                    eng.scalar_tensor_tensor(out=e1_t, in0=iota_f[:, :], scalar=topf_close(t)[:, 0:1], in1=wide_close(t, EX),
                                             op0=ALU.is_equal, op1=ALU.mult).then_inc(made, 1)
                elif part == 1:
                    eng.scalar_tensor_tensor(out=e2_t, in0=iota_f[:, :], scalar=topf_close(t)[:, 1:2], in1=wide_close(t, EX),
                                             op0=ALU.is_equal, op1=ALU.mult).then_inc(made, 1)
                elif part == 2:
                    eng.wait_ge(made, 2)
                    eng.scalar_tensor_tensor(out=em_t, in0=e1_t, scalar=1.0, in1=e2_t, op0=ALU.mult,
                                             op1=ALU.add, accum_out=ga_t[:, 0:1]).then_inc(made, 1)
                elif part == 3:
                    eng.wait_ge(made, 3)
                    eng.scalar_tensor_tensor(out=ga_t[:, 1:2], in0=sum_close(t), scalar=GATE_EPS, in1=ga_t[:, 0:1],
                                             op0=ALU.mult, op1=ALU.add).then_inc(made, 1)
                elif part == 4:
                    eng.scalar_tensor_tensor(out=wide_close(t, GSC), in0=em_t, scalar=1.0, in1=aw[:, :], op0=ALU.mult,
                                             op1=ALU.mult, accum_out=ga_t[:, 3:4]).then_inc(made, 1)
                elif part == 5:
                    eng.wait_ge(made, 5)
                    eng.reciprocal(ga_t[:, 2:3], ga_t[:, 1:2]).then_inc(made, 1)
                elif part == 6:
                    eng.wait_ge(made, 6)
                    eng.tensor_scalar(ga_t[:, 4:5], ga_t[:, 3:4], ga_t[:, 2:3], 0.2, ALU.mult, ALU.mult).then_inc(made, 1)
                elif part == 7:
                    eng.wait_ge(made, 7)
                    eng.tensor_scalar(ga_t[:, 5:6], ga_t[:, 4:5], 0.9, ga_t[:, 2:3], ALU.add, ALU.mult).then_inc(made, 1)
                elif part == 8:
                    eng.wait_ge(made, 8)
                    eng.tensor_scalar(wide_close(t, GW), em_t, ga_t[:, 5:6], gf[:, :], ALU.mult, ALU.mult).then_inc(made, 1)
                else:
                    eng.wait_ge(made, 9)
                    eng.wait_ge(cl_hu, t + 1)
                    eng.tensor_tensor(hug_close[:, t, :].rearrange("p (s r) -> p s r", r=R),
                                      p_scan[:, t, :].rearrange("p (s r) -> p s r", r=R),
                                      wide_close(t, GW).unsqueeze(2).to_broadcast([P, S, R]), ALU.mult).then_inc(cl_hug, 1)

            eng.wait_ge(ac_turn, START + turns_before(CLOSING) - 1)
            residual_close(0, 0)
            accumulate(B - 1, Q - 1, NB - 1, 2)
            residual_close(0, 1)
            accumulate(B - 1, Q - 1, NB - 1, 3)
            for t, part in [(0, 2), (1, 0), (0, 3), (1, 1), (1, 2), (2, 0), (3, 0), (2, 1), (1, 3), (2, 2),
                            (3, 1), (2, 3), (3, 2), (3, 3)]:
                residual_close(t, part)
            for pair in [(0, 1), (2, 3)]:
                for part in range(4):
                    for t in pair:
                        top_two_close(t, part)
                for part in range(10):
                    for t in pair:
                        gates_close(t, part)
            for t in range(Q):
                eng.wait_ge(cl_v, t + 1)
                eng.tensor_tensor(ot_close[:, t, :], p_scan[:, t, :], x2_close[:, t, :], ALU.add).then_inc(cl_out, 1)


def kernel(**inputs):
    import numpy as _np
    import concourse.bacc as _bacc
    from concourse import mybir as _mybir
    from concourse.bass_utils import run_bass_kernel_spmd as _run

    given = {k: _np.asarray(a) for k, a in inputs.items()}
    s, hdim, r = given["L0_ffn_U"].shape
    arrays = {
        "x": given["x"],
        "ctx_t": given["ctx_1024"].transpose(0, 2, 1),
        "g_xattn": given["g_xattn"],
        "g_ffn": given["g_ffn"],
        "in_w_t": given["L0_xattn_in_proj_w"].T,
        "conv_w": given["L0_xattn_conv_w"],
        "conv_b": given["L0_xattn_conv_b"],
        "x_w_t": given["L0_xattn_x_proj_w"].T,
        "dt_w_t": given["L0_xattn_dt_proj_w"].T,
        "dt_b": given["L0_xattn_dt_proj_b"],
        "a_log": given["L0_xattn_A_log"],
        "d_skip": given["L0_xattn_D"],
        "router_t": given["L0_ffn_Wr"].T,
        "u_w": given["L0_ffn_U"].transpose(1, 0, 2).reshape(hdim, s * r),
        "v_w": given["L0_ffn_V"].reshape(s * r, hdim),
        "attr_t": given["L0_ffn_attr"].T,
        "attr_w": given["L0_ffn_Wa"],
    }
    nc = _bacc.Bacc("TRN2", target_bir_lowering=False, num_devices=1)
    maps, args = {}, []
    for name, a in arrays.items():
        a = _np.ascontiguousarray(a)
        maps[f"in_{name}"] = a
        args.append(nc.dram_tensor(f"in_{name}", a.shape, _mybir.dt.from_np(a.dtype), kind="ExternalInput").ap())
    args.append(nc.dram_tensor("out_0", given["x"].shape, _mybir.dt.float32, kind="ExternalOutput").ap())
    flamingo(nc, *args)
    got = _run(nc, [maps], core_ids=[0])
    return got.results[0]["out_0"]
```
